# Optimizing a Trainium2 kernel written in Bass

```python
import numpy as np
import jax
import jax.numpy as jnp

def _softmax(x, axis=-1):
    return jax.nn.softmax(x, axis=axis)

def _gelu(x):
    return jax.nn.gelu(x, approximate=True)

def _silu(x):
    return jax.nn.silu(x)

def _sigmoid(x):
    return jax.nn.sigmoid(x)

def _layernorm(x, axis=-1, eps=1e-05):
    m = jnp.mean(x, axis=axis, keepdims=True)
    v = jnp.var(x, axis=axis, keepdims=True)
    return (x - m) / jnp.sqrt(v + eps)

def _scatter_add(tgt, idx, src, axis=0):
    return tgt.at[idx].add(src)

def _segment_sum(src, seg, n):
    return jax.ops.segment_sum(src, seg, n)
kernel_name = 'mk_xattn_seq_d2_seqx_r8_9f6288'

def setup_inputs(seed: int=0):
    np.random.seed(seed)
    _w = jnp.asarray

    def _rec_inputs():
        import jax
        import jax.numpy as jnp
        _rk = jax.random.key(seed)
        x = 7.22e-05 + 1 * jax.random.normal(jax.random.fold_in(_rk, 1), (8, 128, 256), jnp.float32)
        _lenS = 128 - jax.random.randint(jax.random.fold_in(_rk, 7), (8,), 0, max(1, 128 // 4) + 1, jnp.int32)
        _lenS2 = 128 - jax.random.randint(jax.random.fold_in(_rk, 8), (8,), 0, max(1, 128 // 4) + 1, jnp.int32)
        _ctx_2048P = jax.random.normal(jax.random.fold_in(_rk, 11), (8, 16, 256), jnp.float32)
        _ctx_2048c = jax.random.dirichlet(jax.random.fold_in(_rk, 511), 0.3 * jnp.ones((16,), jnp.float32), (8, 128))
        _ctx_2048t = jnp.einsum('bsk,bkd->bsd', _ctx_2048c, _ctx_2048P)
        _ctx_2048t = _ctx_2048t * jax.lax.rsqrt(jnp.mean(jnp.square(_ctx_2048t)) + 1e-12) * 0.953939
        ctx_2048 = 4.13588e-05 + 0.999923 * (_ctx_2048t + 0.3 * jax.random.normal(jax.random.fold_in(_rk, 611), (8, 128, 256), jnp.float32))
        _validS = jnp.arange(128)[None, :] < _lenS[:, None]
        _validS2 = jnp.arange(128)[None, :] < _lenS2[:, None]
        _causal = jnp.tril(jnp.ones((128, 128), dtype=bool))
        mask_Bx1xSxS2_ff0 = jnp.where(jnp.ones((8, 1, 128, 128), dtype=bool), 0.0, -1000000000.0).astype(jnp.float32)
        mask_BxS2_ik0 = jnp.where(jnp.broadcast_to(_validS2[:, :], (8, 128)), 0, 1).astype(jnp.int32)
        return (x, ctx_2048, mask_Bx1xSxS2_ff0, mask_BxS2_ik0)
    x, ctx_2048, mask_Bx1xSxS2_ff0, mask_BxS2_ik0 = _rec_inputs()

    def _L0_xattn_setup():
        import jax, jax.numpy as jnp
        import numpy as np
        H = 256
        NH = 32
        KVH = 8
        HD = H // NH
        GROUPS = NH // KVH
        EPS = 1e-06
        B, L, S = (4, 128, 128)

        def _gqa_forward(hidden_state, encoder_hidden_state, encoder_attention_mask, Wq, bq, Wk, bk, Wv, bv, Wo, bo, gamma, beta):
            b, l, _ = hidden_state.shape
            s = encoder_hidden_state.shape[1]
            q = hidden_state @ Wq + bq
            k = encoder_hidden_state @ Wk + bk
            v = encoder_hidden_state @ Wv + bv
            q = q.reshape(b, l, KVH, GROUPS, HD).transpose(0, 2, 3, 1, 4)
            k = k.reshape(b, s, KVH, HD).transpose(0, 2, 1, 3)
            v = v.reshape(b, s, KVH, HD).transpose(0, 2, 1, 3)
            scale = 1.0 / jnp.sqrt(jnp.asarray(HD, q.dtype))
            scores = jnp.einsum('bkgld,bksd->bkgls', q, k) * scale
            scores = scores + encoder_attention_mask[:, :, None, :, :]
            attn = jax.nn.softmax(scores, axis=-1)
            out = jnp.einsum('bkgls,bksd->bkgld', attn, v)
            out = out.transpose(0, 3, 1, 2, 4).reshape(b, l, H)
            out = out @ Wo + bo
            x = out + hidden_state
            mu = jnp.mean(x, axis=-1, keepdims=True)
            var = jnp.var(x, axis=-1, keepdims=True)
            return (x - mu) * jax.lax.rsqrt(var + EPS) * gamma + beta
        key = jax.random.key(seed)
        ks = jax.random.split(key, 12)
        sd = 0.02
        return {'hidden_state': jax.random.normal(ks[0], (B, L, H), jnp.float32), 'encoder_hidden_state': jax.random.normal(ks[1], (B, S, H), jnp.float32), 'encoder_attention_mask': jnp.zeros((B, 1, L, S), jnp.float32), 'Wq': jax.random.normal(ks[2], (H, H), jnp.float32) * sd, 'bq': jnp.zeros((H,), jnp.float32), 'Wk': jax.random.normal(ks[3], (H, KVH * HD), jnp.float32) * sd, 'bk': jnp.zeros((KVH * HD,), jnp.float32), 'Wv': jax.random.normal(ks[4], (H, KVH * HD), jnp.float32) * sd, 'bv': jnp.zeros((KVH * HD,), jnp.float32), 'Wo': jax.random.normal(ks[5], (H, H), jnp.float32) * sd, 'bo': jnp.zeros((H,), jnp.float32), 'gamma': jnp.ones((H,), jnp.float32), 'beta': jnp.zeros((H,), jnp.float32)}
    _L0_xattn_all = _L0_xattn_setup()
    _L0_xattn_in = {k: v for k, v in _L0_xattn_all.items() if k in ('Wq', 'bq', 'Wk', 'bk', 'Wv', 'bv', 'Wo', 'bo', 'gamma', 'beta')}
    del _L0_xattn_all

    def _L1_xattn_setup():
        import jax, jax.numpy as jnp
        import numpy as np
        B, P, K, H, NH = (4, 256, 32, 256, 16)
        DH = H // NH
        EPS = 1e-06

        def rmsnorm(x, w):
            var = jnp.mean(jnp.square(x), axis=-1, keepdims=True)
            return x * jax.lax.rsqrt(var + EPS) * w
        key = jax.random.key(seed)
        ks = jax.random.split(key, 12)
        s = 0.02
        return {'x': jax.random.normal(ks[0], (B, P, H), jnp.float32), 'latents': jax.random.normal(ks[1], (B, K, H), jnp.float32), 'attention_mask': jax.random.randint(ks[2], (B, P), 0, 2, jnp.int32), 'q_w': s * jax.random.normal(ks[3], (H, H), jnp.float32), 'q_b': jnp.zeros((H,), jnp.float32), 'kv_w': s * jax.random.normal(ks[4], (H, 2 * H), jnp.float32), 'kv_b': jnp.zeros((2 * H,), jnp.float32), 'out_w': s * jax.random.normal(ks[5], (H, H), jnp.float32), 'out_b': jnp.zeros((H,), jnp.float32), 'postnorm_w': jnp.ones((H,), jnp.float32), 'mlp_w1': s * jax.random.normal(ks[6], (H, 4 * H), jnp.float32), 'mlp_b1': jnp.zeros((4 * H,), jnp.float32), 'mlp_w2': s * jax.random.normal(ks[7], (4 * H, H), jnp.float32), 'mlp_b2': jnp.zeros((H,), jnp.float32)}
    _L1_xattn_all = _L1_xattn_setup()
    _L1_xattn_in = {k: v for k, v in _L1_xattn_all.items() if k in ('q_w', 'q_b', 'kv_w', 'kv_b', 'out_w', 'out_b', 'postnorm_w', 'mlp_w1', 'mlp_b1', 'mlp_w2', 'mlp_b2')}
    del _L1_xattn_all
    return {'x': x, 'ctx_2048': ctx_2048, 'mask_Bx1xSxS2_ff0': mask_Bx1xSxS2_ff0, 'mask_BxS2_ik0': mask_BxS2_ik0, 'L0_xattn_Wq': _L0_xattn_in['Wq'], 'L0_xattn_bq': _L0_xattn_in['bq'], 'L0_xattn_Wk': _L0_xattn_in['Wk'], 'L0_xattn_bk': _L0_xattn_in['bk'], 'L0_xattn_Wv': _L0_xattn_in['Wv'], 'L0_xattn_bv': _L0_xattn_in['bv'], 'L0_xattn_Wo': _L0_xattn_in['Wo'], 'L0_xattn_bo': _L0_xattn_in['bo'], 'L0_xattn_gamma': _L0_xattn_in['gamma'], 'L0_xattn_beta': _L0_xattn_in['beta'], 'L1_xattn_q_w': _L1_xattn_in['q_w'], 'L1_xattn_q_b': _L1_xattn_in['q_b'], 'L1_xattn_kv_w': _L1_xattn_in['kv_w'], 'L1_xattn_kv_b': _L1_xattn_in['kv_b'], 'L1_xattn_out_w': _L1_xattn_in['out_w'], 'L1_xattn_out_b': _L1_xattn_in['out_b'], 'L1_xattn_postnorm_w': _L1_xattn_in['postnorm_w'], 'L1_xattn_mlp_w1': _L1_xattn_in['mlp_w1'], 'L1_xattn_mlp_b1': _L1_xattn_in['mlp_b1'], 'L1_xattn_mlp_w2': _L1_xattn_in['mlp_w2'], 'L1_xattn_mlp_b2': _L1_xattn_in['mlp_b2']}

def reference(x, ctx_2048, mask_Bx1xSxS2_ff0, mask_BxS2_ik0, L0_xattn_Wq, L0_xattn_bq, L0_xattn_Wk, L0_xattn_bk, L0_xattn_Wv, L0_xattn_bv, L0_xattn_Wo, L0_xattn_bo, L0_xattn_gamma, L0_xattn_beta, L1_xattn_q_w, L1_xattn_q_b, L1_xattn_kv_w, L1_xattn_kv_b, L1_xattn_out_w, L1_xattn_out_b, L1_xattn_postnorm_w, L1_xattn_mlp_w1, L1_xattn_mlp_b1, L1_xattn_mlp_w2, L1_xattn_mlp_b2):
    import jax
    import jax.numpy as jnp

    def _L0_xattn_ref(hidden_state, encoder_hidden_state, encoder_attention_mask, Wq, bq, Wk, bk, Wv, bv, Wo, bo, gamma, beta):
        import jax, jax.numpy as jnp
        import numpy as np
        H = 256
        NH = 32
        KVH = 8
        HD = H // NH
        GROUPS = NH // KVH
        EPS = 1e-06
        B, L, S = (4, 128, 128)

        def _gqa_forward(hidden_state, encoder_hidden_state, encoder_attention_mask, Wq, bq, Wk, bk, Wv, bv, Wo, bo, gamma, beta):
            b, l, _ = hidden_state.shape
            s = encoder_hidden_state.shape[1]
            q = hidden_state @ Wq + bq
            k = encoder_hidden_state @ Wk + bk
            v = encoder_hidden_state @ Wv + bv
            q = q.reshape(b, l, KVH, GROUPS, HD).transpose(0, 2, 3, 1, 4)
            k = k.reshape(b, s, KVH, HD).transpose(0, 2, 1, 3)
            v = v.reshape(b, s, KVH, HD).transpose(0, 2, 1, 3)
            scale = 1.0 / jnp.sqrt(jnp.asarray(HD, q.dtype))
            scores = jnp.einsum('bkgld,bksd->bkgls', q, k) * scale
            scores = scores + encoder_attention_mask[:, :, None, :, :]
            attn = jax.nn.softmax(scores, axis=-1)
            out = jnp.einsum('bkgls,bksd->bkgld', attn, v)
            out = out.transpose(0, 3, 1, 2, 4).reshape(b, l, H)
            out = out @ Wo + bo
            x = out + hidden_state
            mu = jnp.mean(x, axis=-1, keepdims=True)
            var = jnp.var(x, axis=-1, keepdims=True)
            return (x - mu) * jax.lax.rsqrt(var + EPS) * gamma + beta
        return _gqa_forward(hidden_state, encoder_hidden_state, encoder_attention_mask, Wq, bq, Wk, bk, Wv, bv, Wo, bo, gamma, beta)

    def _L1_xattn_ref(x, latents, attention_mask, q_w, q_b, kv_w, kv_b, out_w, out_b, postnorm_w, mlp_w1, mlp_b1, mlp_w2, mlp_b2):
        import jax, jax.numpy as jnp
        import numpy as np
        B, P, K, H, NH = (4, 256, 32, 256, 16)
        DH = H // NH
        EPS = 1e-06

        def rmsnorm(x, w):
            var = jnp.mean(jnp.square(x), axis=-1, keepdims=True)
            return x * jax.lax.rsqrt(var + EPS) * w
        b, p, _ = x.shape
        k_len = latents.shape[1]
        residual = latents
        h = jnp.concatenate([x, latents], axis=1)
        q = (latents @ q_w + q_b).reshape(b, k_len, NH, DH)
        kv = (h @ kv_w + kv_b).reshape(b, p + k_len, NH, DH, 2)
        kmat, v = (kv[..., 0], kv[..., 1])
        attn = jnp.einsum('bkhd,bnhd->bhkn', q, kmat) / DH
        full_mask = jnp.concatenate([attention_mask.astype(bool), jnp.ones((b, k_len), bool)], axis=-1)
        attn = jnp.where(full_mask[:, None, None, :], attn, -jnp.inf)
        attn = jax.nn.softmax(attn.astype(jnp.float32), axis=-1).astype(q.dtype)
        attn_out = jnp.einsum('bhkn,bnhd->bkhd', attn, v).reshape(b, k_len, H)
        attn_out = attn_out @ out_w + out_b + residual
        out = rmsnorm(attn_out, postnorm_w)
        out = jax.nn.gelu(out @ mlp_w1 + mlp_b1) @ mlp_w2 + mlp_b2
        return out + residual
    x = _L0_xattn_ref(x, ctx_2048, mask_Bx1xSxS2_ff0, L0_xattn_Wq, L0_xattn_bq, L0_xattn_Wk, L0_xattn_bk, L0_xattn_Wv, L0_xattn_bv, L0_xattn_Wo, L0_xattn_bo, L0_xattn_gamma, L0_xattn_beta)
    x = _L1_xattn_ref(ctx_2048, x, mask_BxS2_ik0, L1_xattn_q_w, L1_xattn_q_b, L1_xattn_kv_w, L1_xattn_kv_b, L1_xattn_out_w, L1_xattn_out_b, L1_xattn_postnorm_w, L1_xattn_mlp_w1, L1_xattn_mlp_b1, L1_xattn_mlp_w2, L1_xattn_mlp_b2)
    return x

_drawn_inputs = setup_inputs


def setup_inputs(seed=0):
    import zlib

    import numpy as np

    out = dict(_drawn_inputs(seed))
    spreads = {'L0_xattn_bq': (0.0, 0.8),
     'L0_xattn_bk': (0.0, 0.8),
     'L0_xattn_bv': (0.0, 0.1),
     'L0_xattn_bo': (0.0, 0.1),
     'L0_xattn_gamma': (1.0, 0.2),
     'L0_xattn_beta': (0.0, 0.1),
     'L1_xattn_q_b': (0.0, 0.8),
     'L1_xattn_kv_b': (0.0, 0.8),
     'L1_xattn_out_b': (0.0, 0.8),
     'L1_xattn_postnorm_w': (1.0, 0.6),
     'L1_xattn_mlp_b1': (0.0, 0.1),
     'L1_xattn_mlp_b2': (0.0, 0.1)}
    factors = {'L0_xattn_Wq': 8.0,
     'L0_xattn_Wk': 8.0,
     'L1_xattn_q_w': 8.0,
     'L1_xattn_kv_w': 8.0,
     'L1_xattn_out_w': 8.0}
    for name, (base, spread) in spreads.items():
        noise = np.random.default_rng([zlib.crc32(name.encode()), seed]).standard_normal(out[name].shape)
        drawn = base * np.exp(spread * noise) if base else spread * noise
        out[name] = jnp.asarray(drawn.astype(out[name].dtype))
    for name, factor in factors.items():
        out[name] = (out[name] * factor).astype(out[name].dtype)
    return out
```

```python
from contextlib import ExitStack

import concourse.bass as bass
from concourse import mybir

F32 = mybir.dt.float32
BF16 = mybir.dt.bfloat16
I32 = mybir.dt.int32
ALU = mybir.AluOpType
ACT = mybir.ActivationFunctionType
AX = mybir.AxisListType

NB, S, H = 8, 128, 256
T = NB * S
HC = H // 128
NH0, KV0, D0 = 32, 8, 8
G0 = NH0 // KV0
NH1, D1 = 16, 16
F = 4 * H
FC = F // 128
SCALE0 = float(D0) ** -0.5
SCALE1 = 1.0 / D1
EPS = 1e-6
BANKS = 8
LOWEST = -3.0e38
MASKED = -1.0e30
UNITS = 2 * NB
MASK_ROW, MAX_ROW, ROWS = 96, 97, 100
PAIRS = ((0, 0, 3), (3, 1, 2), (5, 2, 1))
STORED0 = 3 * 16 + 2 * 48
JOBS0 = 10


def cross_attention_layers(nc, xT, x, cT, mask, key_mask, wq0, bq0, wk0, bk0, wv0, bv0, wo0, bo0, gamma, beta,
                           wq1, bq1, wk1, bk1, wv1, bv1, wo1, bo1, post_w, w1, b1, w2, b2, out):
    ctx = ExitStack()
    with ctx:
        def sb(name, shape, dt=F32):
            return ctx.enter_context(nc.sbuf_tensor(name, shape, dt))

        def bank(name):
            return ctx.enter_context(nc.psum_tensor(name, [128, 512], F32))

        def sem(name):
            return ctx.enter_context(nc.semaphore(name))

        q0_parts = nc.dram_tensor("q0_parts", [2, 3, NB // 2, H, S], BF16, kind="Internal").ap()
        k0_parts = nc.dram_tensor("k0_parts", [2, 3, NB // 2, KV0 * D0, S], BF16, kind="Internal").ap()
        q1_parts = nc.dram_tensor("q1_parts", [NB, 3, H, S], BF16, kind="Internal").ap()
        k1_parts = nc.dram_tensor("k1_parts", [NB, 2, 3, H, S], BF16, kind="Internal").ap()
        key_bias_dram = nc.dram_tensor("key_bias_dram", [NB, S], BF16, kind="Internal").ap()

        q_stack = sb("q_stack", [128, 2, NH0 * S], BF16)
        k_stack = sb("k_stack", [128, 2, 2 * NH1 * S], BF16)
        probs = sb("probs", [128, 2, BANKS * 512])
        x_cols = probs[:, 1, 0:HC * T].rearrange("p (c t) -> p c t", c=HC)
        c_cols = probs[:, 1, HC * T:2 * HC * T].rearrange("p (c t) -> p c t", c=HC)
        wq0_sb, wo0_sb = sb("wq0_sb", [128, HC, H]), sb("wo0_sb", [128, HC, H])
        wk0_sb = sb("wk0_sb", [128, HC, KV0 * D0])
        wv_sb = sb("wv_sb", [128, HC, KV0 * D0 + H])
        wq1_sb, wk1_sb, wo1_sb = (sb(n, [128, HC, H]) for n in ("wq1_sb", "wk1_sb", "wo1_sb"))
        w1_sb, w2_sb = sb("w1_sb", [128, HC, F]), sb("w2_sb", [128, FC, H])
        bq0_sb, bq1_sb, bk1_sb = (sb(n, [128, HC]) for n in ("bq0_sb", "bq1_sb", "bk1_sb"))
        bk0_sb, b1_sb = sb("bk0_sb", [KV0 * D0, 1]), sb("b1_sb", [128, FC])
        bv_row = sb("bv_row", [128, KV0 * D0 + H])
        bo0_row, gamma_row, beta_row, bo1_row, post_row, b2_row = (
            sb(n, [128, H]) for n in ("bo0_row", "gamma_row", "beta_row", "bo1_row", "post_row", "b2_row"))
        ident = sb("ident", [128, 128])
        minus_half = sb("minus_half", [128, 1])
        key_mask_sb = sb("key_mask_sb", [NB, S], I32)
        key_bias = sb("key_bias", [NB, S], BF16)
        staged = sb("staged", [128, 2, 512])
        rest = sb("rest", [128, 2, 512])
        part_store = sb("part_store", [128, 2, 3 * 512], BF16)
        parts = part_store[:, :, :].rearrange("c n (p x) -> c n p x", p=3)
        parts_lat = part_store[:, :, 0:3 * H].rearrange("c n (p x) -> c n p x", p=3)
        v_ctx = sb("v_ctx", [128, NB, KV0 * D0 + H])
        v_lat = sb("v_lat", [128, NB, H])
        v0_ones = sb("v0_ones", [128, 2, KV0, 32])
        v1_ones = sb("v1_ones", [128, 2, 2, NH1, 32])
        mask_sb = sb("mask_sb", [128, 2, S])
        resid0 = sb("resid0", [128, 2, H])
        row_max = sb("row_max", [128, 2, NH0])
        neg_max, neg_rest = sb("neg_max", [NH0, S]), sb("neg_rest", [NH0, S])
        max_parts = sb("max_parts", [NH0, 3, S], BF16)
        o_cols = sb("o_cols", [128, 2, 512])
        inv_sum = sb("inv_sum", [128, 2, 16])
        attn = sb("attn", [128, H])
        attn_cols = sb("attn_cols", [128, HC, S])
        y, y_scaled = sb("y", [128, H]), sb("y_scaled", [128, H])
        stats, mean_var = sb("stats", [128, 6]), sb("mean_var", [128, 2])
        mean_sq, spread, inv_std = sb("mean_sq", [128, 1]), sb("spread", [128, 1]), sb("inv_std", [128, 1])
        normed = sb("normed", [128, 2, H])
        latent_cols = sb("latent_cols", [128, HC, S])
        resid1 = sb("resid1", [128, NB, H])
        resid2 = sb("resid2", [128, NB, H])
        normed_cols = sb("normed_cols", [128, HC, T])
        result = sb("result", [128, 2, H])

        s1_bank = [bank("s1_bank0"), bank("s1_bank1")]
        s2_bank = [bank("s2_bank0"), bank("s2_bank1")]
        pv_bank, ot_bank = bank("pv_bank"), bank("ot_bank")
        m0_bank, m1_bank = bank("m0_bank"), bank("m1_bank")
        job_bank = [s2_bank[0], s2_bank[1], pv_bank, ot_bank]

        ld_wq0, ld_wk0, ld_wk1, ld_wv = (sem(n) for n in ("ld_wq0", "ld_wk0", "ld_wk1", "ld_wv"))
        ld_x = [sem("ld_x0"), sem("ld_x1")]
        ld_c = [sem("ld_c0"), sem("ld_c1")]
        ld_bias, ld_rows, ld_wo0, ld_w1l, ld_mlp, ld_keym = (sem(n) for n in (
            "ld_bias", "ld_rows", "ld_wo0", "ld_w1l", "ld_mlp", "ld_keym"))
        consts, bias_scaled, stacks_init, zeroed = sem("consts"), sem("bias_scaled"), sem("stacks_init"), sem("zeroed")
        key_bias_ready, key_bias_stored = sem("key_bias_ready"), sem("key_bias_stored")
        job_mm, job_staged, job_rest, job_mid, job_split = (sem(n) for n in (
            "job_mm", "job_staged", "job_rest", "job_mid", "job_split"))
        job_stored = [sem("job_stored0"), sem("job_stored1")]
        vctx_mm, vctx_sb, vlat_mm, vlat_sb, v_ready = (sem(n) for n in (
            "vctx_mm", "vctx_sb", "vlat_mm", "vlat_sb", "v_ready"))
        stack_ld = [[sem(f"stack_ld{par}{half}") for half in range(2)] for par in range(2)]
        mask_ld = [sem("mask_ld0"), sem("mask_ld1")]
        resid_ld = [sem("resid_ld0"), sem("resid_ld1")]
        resid0_ready = sem("resid0_ready")
        s1_ready, max_ready, maxT_ready, neg_ready, neg_rest_ready, neg_mid_ready, max_split = (sem(n) for n in (
            "s1_ready", "max_ready", "maxT_ready", "neg_ready", "neg_rest_ready", "neg_mid_ready", "max_split"))
        max_rows = sem("max_rows")
        s2_ready, p_ready, pv_ready, o_sb, oT_ready, inv_ready, attn_ready = (sem(n) for n in (
            "s2_ready", "p_ready", "pv_ready", "o_sb", "oT_ready", "inv_ready", "attn_ready"))
        attnT_ready, attnT_sb, wo_ready, y_ready, moments, spread_ready, std_ready = (sem(n) for n in (
            "attnT_ready", "attnT_sb", "wo_ready", "y_ready", "moments", "spread_ready", "std_ready"))
        bn_done, scaled_ready, normed_ready, resid12_ready = (sem(n) for n in (
            "bn_done", "scaled_ready", "normed_ready", "resid12_ready"))
        xT_ready, xT_sb = sem("xT_ready"), sem("xT_sb")
        h_mm, h_ready, mlp_mm, result_ready = sem("h_mm"), sem("h_ready"), sem("mlp_mm"), sem("result_ready")
        stored = [sem("stored0"), sem("stored1")]
        passed, stacks_ones = sem("passed"), sem("stacks_ones")
        rows_one, rows_set, query_row_set = sem("rows_one"), sem("rows_set"), sem("query_row_set")

        def iterate(eng, step):
            for i in (-1, 0, 1):
                step(i, i % 2, layers(i))
            with eng.Fori(0, 2) as pair:
                step(pair * 2 + 2, 0, layers(2))
                step(pair * 2 + 3, 1, layers(3))
            for i in (6, 7, 8, 9):
                step(i, i % 2, layers(i))
            with eng.Fori(0, 2) as pair:
                step(pair * 2 + 10, 0, layers(10))
                step(pair * 2 + 11, 1, layers(11))
            for i in (14, 15, 16, 17):
                step(i, i % 2, layers(i))

        def layers(i):
            return [(u // NB if 0 <= u < UNITS else None) for u in (i + 1, i, i - 1, i - 2, i + 2)]

        def need(eng, semaphore, count):
            if not isinstance(count, int) or count > 0:
                eng.wait_ge(semaphore, count)

        def alone(eng):
            eng.sem_inc(passed, 1)

        def at(u, size=1):
            return bass.ds(u, size)

        def stack_need(eng, u, par, layer, half):
            if layer == 0:
                n = (u - par) * (16 * 6 // 2) + 16 * 6
            else:
                n = (u - par - NB) * (16 * 7 // 2) + (16 * 6 * NB // 2 + 16 * 7)
            need(eng, stack_ld[par][half], n)

        block = ctx.enter_context(nc.Block())

        @block.sync
        def _(sp):
            sp.dma_start(wq0_sb[:, :, :], wq0).then_inc(ld_wq0, 16)
            for half in range(2):
                sp.dma_start(x_cols[:, :, half * 512:(half + 1) * 512], xT[:, :, half * 512:(half + 1) * 512]).then_inc(ld_x[half], 16)
                if half == 0:
                    sp.dma_start(bq0_sb[:, :], bq0).then_inc(ld_bias, 16)
                    sp.dma_start(bk0_sb[:, :], bk0).then_inc(ld_bias, 16)
                    sp.dma_start(bq1_sb[:, :], bq1).then_inc(ld_bias, 16)
                    sp.dma_start(bk1_sb[:, :], bk1).then_inc(ld_bias, 16)
                    sp.dma_start(wk0_sb[:, :, :], wk0).then_inc(ld_wk0, 16)
                sp.dma_start(c_cols[:, :, half * 512:(half + 1) * 512], cT[:, :, half * 512:(half + 1) * 512]).then_inc(ld_c[half], 16)
            sp.dma_start(wk1_sb[:, :, :], wk1).then_inc(ld_wk1, 16)
            sp.dma_start(wv_sb[:, :, 0:KV0 * D0], wv0).then_inc(ld_wv, 16)
            sp.dma_start(wv_sb[:, :, KV0 * D0:], wv1).then_inc(ld_wv, 16)

            def store_job(j):
                kind, m, half = JOB[j]
                rows = KV0 * D0 if kind == "k0" else 128
                sp.wait_ge(job_split, j + 1)
                src = parts[0:rows, j % 2, :, :]
                if kind == "k1":
                    for p in range(3):
                        sp.dma_start(k1_parts[4 * half:4 * half + 4, 0, p, m * 128:(m + 1) * 128, :].rearrange("b c t -> c b t"),
                                     src[:, p, :].rearrange("c (b t) -> c b t", b=4)).then_inc(job_stored[j % 2], 16)
                else:
                    dst = k0_parts[half, :, :, :, :] if kind == "k0" else q0_parts[half, :, :, m * 128:(m + 1) * 128, :]
                    sp.dma_start(dst.rearrange("p b c t -> c (p b) t"),
                                 src.rearrange("c p (b t) -> c (p b) t", b=4)).then_inc(job_stored[j % 2], 16)

            def store_latents(b):
                for n in range(2):
                    dst = q1_parts[at(b), :, :, :] if n == 0 else k1_parts[at(b), 1, :, :, :]
                    sp.wait_ge(job_split, b * 2 + (JOBS0 + 1 + n))
                    alone(sp)
                    sp.dma_start(dst.rearrange("o p (m c) t -> c (o p m) t", c=128),
                                 parts_lat[:, n, :, :].rearrange("c p (m t) -> c (p m) t", m=HC)).then_inc(job_stored[n], 16)

            def load_stack(v, par, layer, half):
                first_of_layer1 = isinstance(v, int) and v in (NB, NB + 1)
                need(sp, s2_ready, (v - 1) * BANKS if first_of_layer1 else (v - 2) * BANKS + 4 * (half + 1))
                alone(sp)
                if layer == 0:
                    early = isinstance(v, int) and v < 4
                    sp.wait_ge(job_stored[0], 16 * (2 if early else 3))
                    sp.wait_ge(job_stored[1], 16 * (1 if early else 3))
                    alone(sp)
                    qn, kn = 16 * S, 4 * S
                    which = 0 if early else 1
                    for first, part, n in PAIRS:
                        src = q0_parts[which, part:part + 1, at(v - 4 * which), :, :].rearrange("o c (d h) t -> (o c) d (h t)", d=D0)
                        sp.dma_start(q_stack[first * D0:(first + n) * D0, par, half * qn:(half + 1) * qn],
                                     src[:, :, half * qn:(half + 1) * qn].broadcast_to([n, D0, qn])).then_inc(stack_ld[par][half], 16)
                        src = k0_parts[which, 0:n, at(v - 4 * which), :, :].rearrange("c o (d h) t -> (o c) d (h t)", d=D0)
                        sp.dma_start(k_stack[first * D0:(first + n) * D0, par, half * kn:(half + 1) * kn],
                                     src[:, :, half * kn:(half + 1) * kn]).then_inc(stack_ld[par][half], 16)
                else:
                    b = v - NB
                    sp.wait_ge(rows_set, 2)
                    sp.wait_ge(job_stored[0], b * 16 + (STORED0 + 16))
                    sp.wait_ge(job_stored[1], b * 16 + (STORED0 + 16))
                    alone(sp)
                    n8 = 8 * S
                    k_halves = k_stack[:, par, :].rearrange("r (c x) -> r c x", c=2)
                    for first, part, n in PAIRS:
                        src = q1_parts[at(b), part:part + 1, :, :].rearrange("o c (d h) t -> (o c) d (h t)", d=D1)
                        sp.dma_start(q_stack[first * D1:(first + n) * D1, par, half * n8:(half + 1) * n8],
                                     src[:, :, half * n8:(half + 1) * n8].broadcast_to([n, D1, n8])).then_inc(stack_ld[par][half], 16)
                        src = k1_parts[at(b), :, 0:n, :, :].rearrange("o a c (d h) t -> (o c) d a (h t)", d=D1)
                        sp.dma_start(k_halves[first * D1:(first + n) * D1, :, half * n8:(half + 1) * n8],
                                     src[:, :, :, half * n8:(half + 1) * n8]).then_inc(stack_ld[par][half], 16)
                    sp.wait_ge(key_bias_stored, 16)
                    sp.dma_start(k_stack[MASK_ROW:MASK_ROW + 1, par, half * n8:(half + 1) * n8],
                                 key_bias_dram[at(b), :].rearrange("o (a s) -> o a s", a=1).broadcast_to([1, 8, S])).then_inc(stack_ld[par][half], 16)

            def load_mask(v, par):
                need(sp, s2_ready, (v - 1) * BANKS)
                need(sp, max_ready, (v - 1) * BANKS)
                alone(sp)
                sp.dma_start(mask_sb[:, par, :], mask[at(v), :, :].rearrange("o q s -> (o q) s")).then_inc(mask_ld[par], 16)

            for j in range(3):
                store_job(j)
            sp.wait_ge(stacks_init, 1)
            load_stack(0, 0, 0, 0)
            load_mask(0, 0)
            load_stack(0, 0, 0, 1)
            for j in range(3, 6):
                store_job(j)
            sp.dma_start(key_mask_sb[:, :], key_mask).then_inc(ld_keym, 16)
            sp.dma_start(wo0_sb[:, :, :], wo0).then_inc(ld_wo0, 16)
            sp.dma_start(bv_row[:, 0:KV0 * D0], bv0.broadcast_to([128, KV0 * D0])).then_inc(ld_rows, 16)
            sp.dma_start(bv_row[:, KV0 * D0:], bv1.broadcast_to([128, H])).then_inc(ld_rows, 16)
            for row, src in ((bo0_row, bo0), (gamma_row, gamma), (beta_row, beta), (bo1_row, bo1), (post_row, post_w), (b2_row, b2)):
                sp.dma_start(row[:, :], src.broadcast_to([128, H])).then_inc(ld_rows, 16)
            for j in range(6, JOBS0):
                store_job(j)

            def step(i, par, lay):
                l1, l2, lpv, lpr, lld = lay
                if lld is not None:
                    load_stack(i + 2, par, lld, 0)
                if lpr == 0:
                    store_latents(i - 2)
                if l1 is not None:
                    sp.wait_ge(max_split, i + 2)
                    heads = NH1 if l1 else NH0
                    for p in range(3):
                        sp.dma_start(q_stack[MAX_ROW + p:MAX_ROW + p + 1, 1 - par, 0:heads * S],
                                     max_parts[0:heads, p, :]).then_inc(max_rows, 16)
                if lld is not None:
                    load_stack(i + 2, par, lld, 1)
                    if lld == 0:
                        load_mask(i + 2, par)
                if l1 == 0:
                    need(sp, y_ready, i)
                    alone(sp)
                    sp.dma_start(resid0[:, 1 - par, :], x[at(i + 1), :, :].rearrange("o q c -> (o q) c")).then_inc(resid_ld[1 - par], 16)
                if i_is(i, -1):
                    sp.wait_ge(key_bias_ready, 1)
                    sp.dma_start(key_bias_dram, key_bias[:, :]).then_inc(key_bias_stored, 16)
                    sp.dma_start(wq1_sb[:, :, :], wq1).then_inc(ld_w1l, 16)
                    sp.dma_start(wo1_sb[:, :, :], wo1).then_inc(ld_w1l, 16)
                if i_is(i, 0):
                    sp.dma_start(w1_sb[:, :, :], w1).then_inc(ld_mlp, 16)
                    sp.dma_start(b1_sb[:, :], b1).then_inc(ld_mlp, 16)
                    sp.dma_start(w2_sb[:, :, :], w2).then_inc(ld_mlp, 16)

            iterate(sp, step)
            for b in range(NB):
                sp.wait_ge(result_ready, b + 1)
                sp.dma_start(out[b], result[:, b % 2, :]).then_inc(stored[b % 2], 16)
            for par in range(2):
                sp.wait_ge(stored[par], 16 * NB // 2)

        @block.gpsimd
        def _(pool):
            pool.sem_inc(resid12_ready, 1)
            pool.memset(ident[:, :], 0.0).then_inc(zeroed, 1)
            pool.wait_ge(zeroed, 1)
            pool.affine_select(out=ident[:, :], in_=ident[:, :], compare_op=ALU.not_equal, fill=1.0,
                               base=0, pattern=[[-1, 128]], channel_multiplier=1).then_inc(consts, 1)
            pool.wait_ge(ld_bias, 64)
            pool.tensor_scalar(bq0_sb[:, :], bq0_sb[:, :], SCALE0, None, ALU.mult).then_inc(bias_scaled, 1)
            pool.tensor_scalar(bq1_sb[:, :], bq1_sb[:, :], SCALE1, None, ALU.mult).then_inc(bias_scaled, 1)
            pool.memset(minus_half[:, :], -0.5).then_inc(consts, 1)
            pool.memset(v0_ones[:, :, :, :], 1.0).then_inc(consts, 1)
            pool.memset(v1_ones[:, :, :, :, :], 1.0).then_inc(consts, 1)
            pool.wait_ge(consts, 4)
            pool.wait_ge(ld_rows, 128)

            def step(i, par, lay):
                l1, l2, lpv, lpr, lld = lay
                if l2 is not None:
                    need(pool, pv_ready, (i - 1) * 2)
                    alone(pool)
                    if l2 == 0:
                        pool.wait_ge(vctx_sb, NB)
                        pool.tensor_copy(v0_ones[:, par, :, 0:D0],
                                         v_ctx[:, at(i), 0:KV0 * D0].rearrange("p o (k d) -> p (o k) d", d=D0)).then_inc(v_ready, 1)
                    else:
                        pool.tensor_copy(v1_ones[:, par, 0, :, 0:D1],
                                         v_ctx[:, at(i - NB), KV0 * D0:].rearrange("p o (k d) -> p (o k) d", d=D1))
                        pool.wait_ge(vlat_sb, i - NB + 1)
                        alone(pool)
                        pool.tensor_copy(v1_ones[:, par, 1, :, 0:D1],
                                         v_lat[:, at(i - NB), :].rearrange("p o (k d) -> p (o k) d", d=D1)).then_inc(v_ready, 1)
                if lpr == 0:
                    for n in range(2):
                        j = (i - 2) * 2 + JOBS0 + n
                        pool.wait_ge(job_rest, j + 1)
                        alone(pool)
                        pool.tensor_copy(parts_lat[:, n, 1, :], rest[:, n, 0:H]).then_inc(job_mid, 1)
                        pool.wait_ge(job_mid, j + 1)
                        pool.tensor_tensor(parts_lat[:, n, 2, :], rest[:, n, 0:H], parts_lat[:, n, 1, :], ALU.subtract).then_inc(job_split, 1)
                if lpv == 0:
                    pool.wait_ge(resid_ld[1 - par], (i - 1 - (1 - par)) * 8 + 16)
                    pool.tensor_tensor(resid0[:, 1 - par, :], resid0[:, 1 - par, :], bo0_row[:, :], ALU.add).then_inc(resid0_ready, 1)
                if lpv is not None:
                    pool.wait_ge(moments, i)
                    alone(pool)
                    if lpv == 0:
                        pool.tensor_scalar(spread[:, :], mean_var[:, 1:2], EPS, None, ALU.add).then_inc(spread_ready, 1)
                    else:
                        pool.tensor_scalar(spread[:, :], mean_sq[:, :], 1.0 / H, EPS, ALU.mult, ALU.add).then_inc(spread_ready, 1)
                    pool.wait_ge(spread_ready, i)
                    pool.tensor_tensor(inv_std[:, :], spread[:, :], minus_half[:, :], ALU.pow).then_inc(std_ready, 1)
                if lpv == 0:
                    pool.wait_ge(normed_ready, i)
                    for resid, row in ((resid1, bo1_row), (resid2, b2_row)):
                        pool.tensor_tensor(resid[:, at(i - 1), :].rearrange("p o c -> p (o c)"), normed[:, 1 - par, :],
                                           row[:, :], ALU.add).then_inc(resid12_ready, 1)

            iterate(pool, step)

        @block.tensor
        def _(pe):
            def project(out_ap, w, cols, m, n):
                for c in range(HC):
                    mm = pe.matmul(out_ap, w[:, c, m * 128:m * 128 + n], cols(c), start=(c == 0), stop=(c == HC - 1))
                return mm

            def job(j):
                kind, m, half = JOB[j]
                pe.wait_ge({"q0": ld_wq0, "k0": ld_wk0, "k1": ld_wk1}[kind], 16)
                pe.wait_ge((ld_x if kind == "q0" else ld_c)[half], 16)
                need(pe, job_staged, j - 3)
                w = {"q0": wq0_sb, "k0": wk0_sb, "k1": wk1_sb}[kind]
                src = x_cols if kind == "q0" else c_cols
                rows = KV0 * D0 if kind == "k0" else 128
                project(job_bank[j % 4][0:rows, :], w, lambda c: src[:, c, half * 512:(half + 1) * 512], m, rows).then_inc(job_mm, 1)

            def ctx_values(b):
                if b == 0:
                    pe.wait_ge(ld_wv, 32)
                need(pe, vctx_sb, b - 1)
                for c in range(HC):
                    mm = pe.matmul((m0_bank, m1_bank)[b % 2][:, 0:KV0 * D0 + H], c_cols[:, c, b * S:(b + 1) * S], wv_sb[:, c, :],
                                   start=(c == 0), stop=(c == HC - 1))
                mm.then_inc(vctx_mm, 1)

            def pass1(u, par, layer, k):
                if k % 4 == 0:
                    stack_need(pe, u, par, layer, k // 4)
                need(pe, max_ready, u * BANKS + (k - 1))
                dst = s1_bank[k % 2]
                if layer == 0:
                    for g in range(G0):
                        h = k * G0 + g
                        mm = pe.matmul(dst[:, g * S:(g + 1) * S], q_stack[0:MASK_ROW, par, h * S:(h + 1) * S],
                                       k_stack[0:MASK_ROW, par, k * S:(k + 1) * S], start=True, stop=True)
                else:
                    keys = k_stack[0:MAX_ROW, par, :].rearrange("r (c h s) -> r c h s", c=2, h=NH1)
                    for g in range(2):
                        h = 2 * k + g
                        mm = pe.matmul(dst[:, g * 2 * S:(g + 1) * 2 * S].rearrange("p (c s) -> p c s", c=2),
                                       q_stack[0:MAX_ROW, par, h * S:(h + 1) * S], keys[:, :, h, :], start=True, stop=True)
                mm.then_inc(s1_ready, 1)

            def maxima_turned(u, par, layer, lpr):
                heads = NH1 if layer else NH0
                pe.wait_ge(max_ready, u * BANKS + BANKS)
                if isinstance(u, int) and u == 0:
                    pe.wait_ge(consts, 1)
                    pe.wait_ge(vctx_sb, NB)
                if lpr == 0:
                    pe.wait_ge(job_staged, (u - 3) * 2 + JOBS0 + 2)
                elif lpr == 1:
                    pe.wait_ge(xT_sb, u - 2)
                else:
                    need(pe, attnT_sb, u - 2)
                pe.transpose(m0_bank[0:heads, 0:S], row_max[:, par, 0:heads], ident[:, :]).then_inc(maxT_ready, 1)

            def pass2(u, par, layer, k):
                if k == 0:
                    pe.wait_ge(max_rows, u * 48 + 48)
                    if isinstance(u, int) and u == 0:
                        pe.wait_ge(job_staged, JOBS0)
                        pe.wait_ge(query_row_set, 2)
                need(pe, p_ready, u * BANKS + (k - 1))
                dst = s2_bank[k % 2]
                if layer == 0:
                    if k == 0:
                        pe.wait_ge(mask_ld[par], (u - par) * 8 + 16)
                    for g in range(G0):
                        pe.matmul(dst[:, g * S:(g + 1) * S], mask_sb[:, par, :], ident[:, :], is_transpose=True,
                                  start=(g == 0), stop=False)
                    mm = pe.matmul(dst[:, :], k_stack[0:ROWS, par, k * S:(k + 1) * S],
                                   q_stack[0:ROWS, par, k * 512:(k + 1) * 512], start=False, stop=True)
                else:
                    hg, c = k // 2, k % 2
                    for g in range(4):
                        h = 4 * hg + g
                        mm = pe.matmul(dst[:, g * S:(g + 1) * S], k_stack[0:ROWS, par, (c * NH1 + h) * S:(c * NH1 + h + 1) * S],
                                       q_stack[0:ROWS, par, h * S:(h + 1) * S], start=True, stop=True)
                mm.then_inc(s2_ready, 1)

            def values(u, par, layer, half):
                pe.wait_ge(p_ready, u * BANKS + 4 * (half + 1))
                if half == 0:
                    pe.wait_ge(v_ready, u + 1)
                need(pe, o_sb, u * 2 + half)
                if layer == 0:
                    for j in range(4):
                        kv = 4 * half + j
                        mm = pe.matmul(pv_bank[32 * j:32 * j + 32, :], v0_ones[:, par, kv, :], probs[:, par, kv * 512:(kv + 1) * 512],
                                       start=True, stop=True)
                else:
                    for e in range(2):
                        hg = 2 * half + e
                        for c in range(2):
                            for j in range(4):
                                mm = pe.matmul(pv_bank[32 * j:32 * j + 32, e * S:(e + 1) * S], v1_ones[:, par, c, 4 * hg + j, :],
                                               probs[:, par, (2 * hg + c) * 512 + j * S:(2 * hg + c) * 512 + (j + 1) * S],
                                               start=(c == 0), stop=(c == 1))
                mm.then_inc(pv_ready, 1)

            def values_turned(u, layer, half):
                pe.wait_ge(o_sb, u * 2 + half + 1)
                need(pe, attn_ready, u * 2 + half)
                for g in range(2 if layer else 4):
                    mm = pe.transpose(ot_bank[:, g * S:(g + 1) * S], o_cols[:, half, g * S:(g + 1) * S], ident[:, :])
                mm.then_inc(oT_ready, 1)

            def attention_turned(u, more_max):
                pe.wait_ge(attn_ready, u * 2 + 2)
                if more_max:
                    pe.wait_ge(neg_ready, u + 3)
                else:
                    need(pe, xT_sb, u)
                for m in range(HC):
                    mm = pe.transpose(m0_bank[:, m * S:(m + 1) * S], attn[:, m * 128:(m + 1) * 128], ident[:, :])
                mm.then_inc(attnT_ready, 1)

            def out_projection(u, layer, lpr):
                pe.wait_ge(attnT_sb, u + 1)
                pe.wait_ge(ld_w1l if layer else ld_wo0, 32 if layer else 16)
                if lpr == 0:
                    pe.wait_ge(vlat_sb, u)
                elif lpr == 1:
                    pe.wait_ge(y_ready, u)
                w = wo1_sb if layer else wo0_sb
                for c in range(HC):
                    mm = pe.matmul(m1_bank[:, 0:H], attn_cols[:, c, :], w[:, c, :], start=(c == 0), stop=(c == HC - 1))
                mm.then_inc(wo_ready, 1)

            def result_turned(u, par):
                pe.wait_ge(normed_ready, u + 1)
                pe.wait_ge(attnT_sb, u + 1)
                for m in range(HC):
                    mm = pe.transpose(m0_bank[:, m * S:(m + 1) * S], normed[:, par, m * 128:(m + 1) * 128], ident[:, :])
                mm.then_inc(xT_ready, 1)

            def latent_queries(b):
                pe.wait_ge(xT_sb, b + 1)
                pe.wait_ge(ld_w1l, 32)
                need(pe, y_ready, b + 1)
                for m in range(HC):
                    mm = project(m1_bank[:, m * S:(m + 1) * S], wq1_sb, lambda c: latent_cols[:, c, :], m, 128)
                mm.then_inc(job_mm, 1)

            def latent_keys(b):
                for m in range(HC):
                    mm = project(m0_bank[:, m * S:(m + 1) * S], wk1_sb, lambda c: latent_cols[:, c, :], m, 128)
                mm.then_inc(job_mm, 1)

            def latent_values(b):
                pe.wait_ge(job_staged, b * 2 + JOBS0 + 1)
                for c in range(HC):
                    mm = pe.matmul(m1_bank[:, 0:H], latent_cols[:, c, :], wv_sb[:, c, KV0 * D0:], start=(c == 0), stop=(c == HC - 1))
                mm.then_inc(vlat_mm, 1)

            pe.sem_inc(xT_ready, 1)
            pe.sem_inc(vlat_mm, 1)
            for j in range(6):
                job(j)

            def step(i, par, lay):
                l1, l2, lpv, lpr, lld = lay
                for k in range(BANKS):
                    if l2 is not None:
                        pass2(i, par, l2, k)
                    if i_is(i, -1):
                        pass1(0, 0, 0, k)
                        if k < JOBS0 - 6:
                            job(6 + k)
                        ctx_values(k)
                    elif l1 is not None and k < 4:
                        first = 2 * k
                        pass1(i + 1, 1 - par, l1, first)
                        pass1(i + 1, 1 - par, l1, first + 1)
                    if k == 0:
                        if lpr is not None:
                            result_turned(i - 2, par)
                        if lpv is not None:
                            values(i - 1, 1 - par, lpv, 0)
                    if k == 1:
                        if lpv is not None:
                            values_turned(i - 1, lpv, 0)
                        if lpr == 0:
                            latent_queries(i - 2)
                    if k == 2:
                        if lpv is not None:
                            values(i - 1, 1 - par, lpv, 1)
                        if lpr == 0:
                            latent_keys(i - 2)
                    if k == 3:
                        if lpv is not None:
                            values_turned(i - 1, lpv, 1)
                        if lpr == 0:
                            latent_values(i - 2)
                    if k == (7 if i_is(i, -1) else 4) and l1 is not None:
                        maxima_turned(i + 1, 1 - par, l1, lpr)
                    if k == 5 and lpv is not None:
                        attention_turned(i - 1, l1 is not None)
                    if k == 6 and lpv is not None:
                        out_projection(i - 1, lpv, lpr)

            iterate(pe, step)

            pe.wait_ge(ld_mlp, 48)
            pe.wait_ge(xT_sb, UNITS)
            h_bank = [s1_bank[0], s1_bank[1], s2_bank[0], s2_bank[1]]
            for n in range(2 * FC):
                half, m = n // FC, n % FC
                need(pe, h_ready, n - 3)
                if n == 0:
                    pe.wait_ge(max_ready, UNITS * BANKS)
                    pe.wait_ge(p_ready, UNITS * BANKS)
                project(h_bank[n % 4][:, :], w1_sb, lambda c: normed_cols[:, c, half * 512:(half + 1) * 512], m, 128).then_inc(h_mm, 1)
            o_bank = [m0_bank, m1_bank, pv_bank, ot_bank]
            for b in range(NB):
                if b == 0:
                    pe.wait_ge(h_ready, FC)
                    pe.wait_ge(y_ready, UNITS)
                    pe.wait_ge(o_sb, 2 * UNITS)
                    pe.wait_ge(attn_ready, 2 * UNITS)
                if b == NB // 2:
                    pe.wait_ge(h_ready, 2 * FC)
                need(pe, result_ready, b - 3)
                hidden = probs[:, b // 4, :].rearrange("p (m t) -> p m t", m=FC)
                for m in range(FC):
                    mm = pe.matmul(o_bank[b % 4][:, 0:H], hidden[:, m, (b % 4) * S:(b % 4 + 1) * S], w2_sb[:, m, :],
                                   start=(m == 0), stop=(m == FC - 1))
                mm.then_inc(mlp_mm, 1)

        @block.scalar
        def _(act):
            def stage(j):
                kind, m, half = JOB[j]
                rows = KV0 * D0 if kind == "k0" else 128
                if j == 0:
                    act.wait_ge(bias_scaled, 1)
                    act.wait_ge(ld_bias, 64)
                act.wait_ge(job_mm, j + 1)
                need(act, job_split, j - 1)
                need(act, job_stored[j % 2], 16 * min(j // 2, 3) + 48 * max(j // 2 - 3, 0))
                bias = {"q0": bq0_sb[:, m:m + 1], "k0": bk0_sb[:, 0:1], "k1": bk1_sb[:, m:m + 1]}[kind]
                scale = SCALE0 if kind == "q0" else 1.0
                src = job_bank[j % 4][0:rows, :]
                act.activation(staged[0:rows, j % 2, :], src, ACT.Identity, bias=bias, scale=scale)
                act.activation(parts[0:rows, j % 2, 0, :], src, ACT.Identity, bias=bias, scale=scale).then_inc(job_staged, 1)

            def stage_latents(b, n):
                j = b * 2 + (JOBS0 + n)
                act.wait_ge(job_mm, j + 1)
                act.wait_ge(job_split, j - 1)
                act.wait_ge(job_stored[n], b * 16 + STORED0)
                bias, scale = (bq1_sb, SCALE1) if n == 0 else (bk1_sb, 1.0)
                src = (m1_bank, m0_bank)[n]
                for m in range(HC):
                    act.activation(staged[:, n, m * S:(m + 1) * S], src[:, m * S:(m + 1) * S], ACT.Identity,
                                   bias=bias[:, m:m + 1], scale=scale)
                    last = act.activation(parts_lat[:, n, 0, m * S:(m + 1) * S], src[:, m * S:(m + 1) * S], ACT.Identity,
                                          bias=bias[:, m:m + 1], scale=scale)
                last.then_inc(job_staged, 1)

            def negated_maxima(u, layer):
                heads = NH1 if layer else NH0
                act.wait_ge(maxT_ready, u + 1)
                need(act, max_split, u)
                need(act, max_rows, u * 48)
                act.mul(neg_max[0:heads, :], m0_bank[0:heads, 0:S], -1.0)
                act.mul(max_parts[0:heads, 0, :], m0_bank[0:heads, 0:S], -1.0).then_inc(neg_ready, 1)

            def exponentials(u, par, k):
                act.wait_ge(s2_ready, u * BANKS + (k + 1))
                if k % 4 == 0:
                    need(act, pv_ready, (u - 2) * 2 + k // 4 + 1)
                act.activation(probs[:, par, k * 512:(k + 1) * 512], s2_bank[k % 2][:, :], ACT.Exp).then_inc(p_ready, 1)

            def values_out(u, layer, half):
                n = 256 if layer else 512
                act.wait_ge(pv_ready, u * 2 + half + 1)
                need(act, oT_ready, u * 2 + (half - 1))
                act.copy(o_cols[:, half, 0:n], pv_bank[:, 0:n]).then_inc(o_sb, 1)

            def attention_out(u):
                act.wait_ge(attnT_ready, u + 1)
                need(act, wo_ready, u)
                act.copy(attn_cols[:, :, :], m0_bank[:, 0:H].rearrange("p (m t) -> p m t", m=HC)).then_inc(attnT_sb, 1)

            def result_out(u, layer):
                act.wait_ge(xT_ready, u + 2)
                src = m0_bank[:, 0:H].rearrange("p (m t) -> p m t", m=HC)
                if layer == 0:
                    need(act, vlat_mm, u + 1)
                    act.copy(latent_cols[:, :, :], src).then_inc(xT_sb, 1)
                else:
                    act.copy(normed_cols[:, :, bass.ds((u - NB) * S, S)], src).then_inc(xT_sb, 1)

            for j in range(6):
                stage(j)
            act.wait_ge(consts, 1)
            act.wait_ge(stacks_init, 1)
            for par in range(2):
                act.activation(q_stack[MASK_ROW:MASK_ROW + 1, par, 0:NH1 * S], ident[96:97, 0:1].broadcast_to([1, NH1 * S]),
                               ACT.Identity, scale=0.0, bias=1.0).then_inc(query_row_set, 1)

            def constant_rows(par):
                n0, n1 = KV0 * S, 2 * NH1 * S
                some = ident[96:128, 0:1]
                act.activation(k_stack[96:128, par, n0:n1], some.broadcast_to([32, n1 - n0]), ACT.Identity,
                               scale=0.0, bias=1.0).then_inc(rows_one, 1)
                act.wait_ge(rows_one, par + 1)
                act.activation(k_stack[MASK_ROW:MASK_ROW + 1, par, n0:n1], some[0:1].broadcast_to([1, n1 - n0]), ACT.Identity,
                               scale=0.0, bias=0.0).then_inc(rows_set, 1)

            def step(i, par, lay):
                l1, l2, lpv, lpr, lld = lay
                if i_is(i, 0) or i_is(i, 1):
                    constant_rows(par)
                for k in range(BANKS):
                    if l2 is not None:
                        exponentials(i, par, k)
                    if i_is(i, -1) and k < JOBS0 - 6:
                        stage(6 + k)
                    if k == 0:
                        if lpr is not None:
                            result_out(i - 2, lpr)
                        if lpv is not None:
                            values_out(i - 1, lpv, 0)
                    if k == 1 and lpr == 0:
                        stage_latents(i - 2, 0)
                    if k == 2:
                        if lpv is not None:
                            values_out(i - 1, lpv, 1)
                        if lpr == 0:
                            stage_latents(i - 2, 1)
                    if k == (7 if i_is(i, -1) else 4) and l1 is not None:
                        negated_maxima(i + 1, l1)
                    if k == 5 and lpv is not None:
                        attention_out(i - 1)

            iterate(act, step)
            for n in range(2 * FC):
                half, m = n // FC, n % FC
                act.wait_ge(h_mm, n + 1)
                if n == 0:
                    act.wait_ge(pv_ready, 2 * UNITS)
                    act.wait_ge(ld_mlp, 48)
                act.activation(probs[:, half, m * 512:(m + 1) * 512], h_bank_of(n, s1_bank, s2_bank)[:, :], ACT.Gelu_apprx_tanh,
                               bias=b1_sb[:, m:m + 1]).then_inc(h_ready, 1)

        @block.vector
        def _(dve):
            n = KV0 * S
            for par in range(2):
                dve.memset(k_stack[0:96, par, 0:n].bitcast(F32), 0.0)
                last = dve.memset(k_stack[96:128, par, 0:n], 1.0)
            last.then_inc(stacks_ones, 1)
            for par in range(2):
                dve.memset(q_stack[:, par, :].bitcast(F32), 0.0)
            dve.wait_ge(stacks_ones, 1)
            for par in range(2):
                last = dve.memset(k_stack[MASK_ROW:MASK_ROW + 1, par, 0:n].bitcast(F32), 0.0)
            last.then_inc(stacks_init, 1)

            def split(j):
                rows = KV0 * D0 if JOB[j][0] == "k0" else 128
                n = j % 2
                dve.wait_ge(job_staged, j + 1)
                dve.tensor_tensor(rest[0:rows, n, :], staged[0:rows, n, :], parts[0:rows, n, 0, :], ALU.subtract).then_inc(job_rest, 1)
                dve.wait_ge(job_rest, j + 1)
                dve.tensor_copy(parts[0:rows, n, 1, :], rest[0:rows, n, :]).then_inc(job_mid, 1)
                dve.wait_ge(job_mid, j + 1)
                dve.tensor_tensor(parts[0:rows, n, 2, :], rest[0:rows, n, :], parts[0:rows, n, 1, :], ALU.subtract).then_inc(job_split, 1)

            def latent_rest(b, n):
                j = b * 2 + (JOBS0 + n)
                dve.wait_ge(job_staged, j + 1)
                dve.wait_ge(job_split, j - 1)
                dve.tensor_tensor(rest[:, n, 0:H], staged[:, n, 0:H], parts_lat[:, n, 0, :], ALU.subtract).then_inc(job_rest, 1)

            def context_values(b):
                dve.wait_ge(vctx_mm, b + 1)
                if b == 0:
                    dve.wait_ge(ld_rows, 128)
                n = KV0 * D0 + H
                dve.tensor_tensor(v_ctx[:, b, :], (m0_bank, m1_bank)[b % 2][:, 0:n], bv_row[:, :], ALU.add).then_inc(vctx_sb, 1)

            def maxima(u, par, layer, k):
                dve.wait_ge(s1_ready, u * BANKS + (k + 1))
                if k == 0:
                    need(dve, maxT_ready, u - 1)
                    if layer == 0:
                        dve.wait_ge(mask_ld[par], (u - par) * 8 + 16)
                if layer == 0:
                    alone(dve)
                    for g in range(G0):
                        h = k * G0 + g
                        last = dve.tensor_tensor_reduce(s1_bank[k % 2][:, g * S:(g + 1) * S], s1_bank[k % 2][:, g * S:(g + 1) * S], mask_sb[:, par, :],
                                                        1.0, LOWEST, ALU.add, ALU.max, row_max[:, par, h:h + 1])
                    last.then_inc(max_ready, 1)
                else:
                    dve.tensor_reduce(row_max[:, par, 2 * k:2 * k + 2], s1_bank[k % 2][:, :].rearrange("p (h s) -> p h s", h=2),
                                      AX.X, ALU.max).then_inc(max_ready, 1)

            def normalise(u, layer, half):
                dve.wait_ge(oT_ready, u * 2 + half + 1)
                if half == 0:
                    need(dve, attnT_ready, u)
                if layer == 0:
                    turned = ot_bank[:, :].rearrange("q (g j e) -> q j g e", g=G0, j=4)
                    dst = attn[:, half * 128:(half + 1) * 128].rearrange("q (j g d) -> q j g d", j=4, g=G0)
                    d, n = D0, 16
                    inv = inv_sum[:, half, 0:16].rearrange("q (j g a) -> q j g a", j=4, g=G0)
                    shape = [128, 4, G0, D0]
                else:
                    turned = ot_bank[:, 0:2 * S].rearrange("q (e j c) -> q e j c", e=2, j=4)
                    dst = attn[:, half * 128:(half + 1) * 128].rearrange("q (e j d) -> q e j d", e=2, j=4)
                    d, n = D1, 8
                    inv = inv_sum[:, half, 0:8].rearrange("q (e j a) -> q e j a", e=2, j=4)
                    shape = [128, 2, 4, D1]
                dve.reciprocal(inv, turned[:, :, :, d:d + 1]).then_inc(inv_ready, 1)
                dve.wait_ge(inv_ready, u * 2 + half + 1)
                dve.tensor_tensor(dst, turned[:, :, :, 0:d], inv.broadcast_to(shape), ALU.mult).then_inc(attn_ready, 1)

            def residual_sum(u, par, layer):
                dve.wait_ge(wo_ready, u + 1)
                need(dve, normed_ready, u)
                if layer == 0:
                    dve.wait_ge(resid0_ready, u + 1)
                    dve.tensor_tensor(y[:, :], m1_bank[:, 0:H], resid0[:, par, :], ALU.add).then_inc(y_ready, 1)
                    dve.wait_ge(y_ready, u + 1)
                    dve.bn_stats(stats[:, :], y[:, :]).then_inc(bn_done, 1)
                    dve.wait_ge(bn_done, u + 1)
                    alone(dve)
                    dve.bn_aggr(mean_var[:, :], stats[:, :]).then_inc(moments, 1)
                else:
                    dve.wait_ge(resid12_ready, 2 * NB + 1)
                    dve.tensor_tensor(y[:, :], m1_bank[:, 0:H], resid1[:, at(u - NB), :].rearrange("p o c -> p (o c)"), ALU.add).then_inc(y_ready, 1)
                    dve.wait_ge(y_ready, u + 1)
                    dve.tensor_tensor_reduce(y_scaled[:, :], y[:, :], y[:, :], 1.0, 0.0, ALU.mult, ALU.add, mean_sq[:, :]).then_inc(moments, 1)

            def split_maxima(u, layer):
                heads = NH1 if layer else NH0
                dve.wait_ge(neg_ready, u + 1)
                dve.tensor_tensor(neg_rest[0:heads, :], neg_max[0:heads, :], max_parts[0:heads, 0, :], ALU.subtract).then_inc(neg_rest_ready, 1)
                dve.wait_ge(neg_rest_ready, u + 1)
                dve.tensor_copy(max_parts[0:heads, 1, :], neg_rest[0:heads, :]).then_inc(neg_mid_ready, 1)
                dve.wait_ge(neg_mid_ready, u + 1)
                dve.tensor_tensor(max_parts[0:heads, 2, :], neg_rest[0:heads, :], max_parts[0:heads, 1, :], ALU.subtract).then_inc(max_split, 1)

            def norm(u, par, layer):
                dve.wait_ge(std_ready, u + 1)
                need(dve, xT_ready, u)
                if layer == 0:
                    need(dve, resid12_ready, (u - 1) * 2 + 1)
                    dve.scalar_tensor_tensor(y_scaled[:, :], y[:, :], mean_var[:, 0:1], gamma_row[:, :], ALU.subtract, ALU.mult).then_inc(scaled_ready, 1)
                    dve.wait_ge(scaled_ready, u + 1)
                    dve.scalar_tensor_tensor(normed[:, par, :], y_scaled[:, :], inv_std[:, 0:1], beta_row[:, :], ALU.mult, ALU.add).then_inc(normed_ready, 1)
                else:
                    dve.scalar_tensor_tensor(normed[:, par, :], y[:, :], inv_std[:, 0:1], post_row[:, :], ALU.mult, ALU.mult).then_inc(normed_ready, 1)

            for j in range(6):
                split(j)

            def step(i, par, lay):
                l1, l2, lpv, lpr, lld = lay
                for k in range(BANKS):
                    if i_is(i, -1):
                        maxima(0, 0, 0, k)
                        if k < JOBS0 - 6:
                            split(6 + k)
                        context_values(k)
                    elif l1 is not None and k < 4:
                        first = 2 * k
                        maxima(i + 1, 1 - par, l1, first)
                        maxima(i + 1, 1 - par, l1, first + 1)
                    if k == 1 and lpv is not None:
                        normalise(i - 1, lpv, 0)
                    if k == 1 and lpr == 0:
                        latent_rest(i - 2, 0)
                    if k == 2 and lpr == 0:
                        latent_rest(i - 2, 1)
                    if k == 3:
                        if lpv is not None:
                            normalise(i - 1, lpv, 1)
                        if lpr == 0:
                            dve.wait_ge(vlat_mm, i)
                            dve.tensor_tensor(v_lat[:, at(i - 2), :].rearrange("p o c -> p (o c)"), m1_bank[:, 0:H],
                                              bv_row[:, KV0 * D0:], ALU.add).then_inc(vlat_sb, 1)
                    if k == (7 if i_is(i, -1) else 4) and l1 is not None:
                        split_maxima(i + 1, l1)
                    if k == 6 and lpv is not None:
                        residual_sum(i - 1, 1 - par, lpv)
                    if k == 7 and lpv is not None:
                        norm(i - 1, 1 - par, lpv)
                if i_is(i, 0):
                    dve.wait_ge(ld_keym, 16)
                if i_is(i, -1):
                    dve.wait_ge(ld_keym, 16)
                    dve.tensor_scalar(key_bias[:, :], key_mask_sb[:, :], 0.0, MASKED, ALU.is_equal, ALU.mult).then_inc(key_bias_ready, 1)

            iterate(dve, step)
            for b in range(NB):
                dve.wait_ge(mlp_mm, b + 1)
                need(dve, stored[b % 2], 16 * (b // 2))
                dve.tensor_tensor(result[:, b % 2, :], [m0_bank, m1_bank, pv_bank, ot_bank][b % 4][:, 0:H], resid2[:, b, :], ALU.add).then_inc(result_ready, 1)


JOB = [(kind, m, half) for half in range(2) for kind, m in (("q0", 0), ("q0", 1), ("k0", 0))]
JOB += [("k1", m, half) for half in range(2) for m in range(2)]


def i_is(i, n):
    return isinstance(i, int) and i == n


def h_bank_of(n, s1_bank, s2_bank):
    return [s1_bank[0], s1_bank[1], s2_bank[0], s2_bank[1]][n % 4]


def kernel(**inputs):
    import numpy as np
    import concourse.bacc as bacc
    from concourse.bass_utils import run_bass_kernel_spmd

    a = {k: np.asarray(v) for k, v in inputs.items()}

    def cols(w):
        return np.ascontiguousarray(w.reshape(-1, 128, w.shape[1]).transpose(1, 0, 2))

    def tokens(v):
        return cols(v.reshape(T, H).T)

    def d_major(w, heads, d):
        return w.reshape(-1, heads, d).transpose(0, 2, 1).reshape(-1, heads * d)

    kv_w = a["L1_xattn_kv_w"].reshape(H, NH1, D1, 2)
    kv_b = a["L1_xattn_kv_b"].reshape(1, NH1, D1, 2)

    def column(v):
        return cols(v.reshape(-1, 1))[:, :, 0]

    arrays = {
        "xT": tokens(a["x"]), "x": a["x"], "cT": tokens(a["ctx_2048"]),
        "mask": a["mask_Bx1xSxS2_ff0"].reshape(NB, S, S), "key_mask": a["mask_BxS2_ik0"],
        "wq0": cols(d_major(a["L0_xattn_Wq"], NH0, D0)), "bq0": column(d_major(a["L0_xattn_bq"], NH0, D0)),
        "wk0": cols(d_major(a["L0_xattn_Wk"], KV0, D0)), "bk0": d_major(a["L0_xattn_bk"], KV0, D0).reshape(-1, 1),
        "wv0": cols(a["L0_xattn_Wv"]), "bv0": a["L0_xattn_bv"].reshape(1, -1),
        "wo0": cols(a["L0_xattn_Wo"]), "bo0": a["L0_xattn_bo"].reshape(1, -1),
        "gamma": a["L0_xattn_gamma"].reshape(1, -1), "beta": a["L0_xattn_beta"].reshape(1, -1),
        "wq1": cols(d_major(a["L1_xattn_q_w"], NH1, D1)), "bq1": column(d_major(a["L1_xattn_q_b"], NH1, D1)),
        "wk1": cols(d_major(kv_w[..., 0].reshape(H, H), NH1, D1)), "bk1": column(d_major(kv_b[..., 0].reshape(1, H), NH1, D1)),
        "wv1": cols(kv_w[..., 1].reshape(H, H)), "bv1": kv_b[..., 1].reshape(1, H),
        "wo1": cols(a["L1_xattn_out_w"]), "bo1": a["L1_xattn_out_b"].reshape(1, -1),
        "post_w": a["L1_xattn_postnorm_w"].reshape(1, -1),
        "w1": cols(a["L1_xattn_mlp_w1"]), "b1": column(a["L1_xattn_mlp_b1"]),
        "w2": cols(a["L1_xattn_mlp_w2"]), "b2": a["L1_xattn_mlp_b2"].reshape(1, -1),
    }
    nc = bacc.Bacc("TRN2", target_bir_lowering=False, num_devices=1)
    args, feed = [], {}
    for name, v in arrays.items():
        v = np.ascontiguousarray(v)
        feed[f"in_{name}"] = v
        args.append(nc.dram_tensor(f"in_{name}", v.shape, mybir.dt.from_np(v.dtype), kind="ExternalInput").ap())
    out = nc.dram_tensor("out_0", (NB, S, H), F32, kind="ExternalOutput").ap()
    cross_attention_layers(nc, *args, out)
    r = run_bass_kernel_spmd(nc, [feed], core_ids=[0])
    return r.results[0]["out_0"]
```

```python
from contextlib import ExitStack

import concourse.bass as bass
from concourse import mybir

F32 = mybir.dt.float32
BF16 = mybir.dt.bfloat16
I32 = mybir.dt.int32
ALU = mybir.AluOpType
ACT = mybir.ActivationFunctionType
AX = mybir.AxisListType

NB, S, H = 8, 128, 256
T = NB * S
HC = H // 128
NH0, KV0, D0 = 32, 8, 8
G0 = NH0 // KV0
NH1, D1 = 16, 16
F = 4 * H
FC = F // 128
SCALE0 = float(D0) ** -0.5
SCALE1 = 1.0 / D1
EPS = 1e-6
BANKS = 8
LOWEST = -3.0e38
MASKED = -1.0e30
UNITS = 2 * NB
MASK_ROW, MAX_ROW, ROWS = 96, 97, 100
HALF_COL1 = (8 * S, 0)
PAIRS = ((0, 0, 3), (3, 1, 2), (5, 2, 1))
STORED0 = 3 * 16 + 2 * 48
JOBS0 = 10


def cross_attention_layers(nc, xT, x, cT, mask, key_mask, wq0, bq0, wk0, bk0, wv0, bv0, wo0, bo0, gamma, beta,
                           wq1, bq1, wk1, bk1, wv1, bv1, wo1, bo1, post_w, w1, b1, w2, b2, out):
    ctx = ExitStack()
    with ctx:
        def sb(name, shape, dt=F32):
            return ctx.enter_context(nc.sbuf_tensor(name, shape, dt))

        def bank(name):
            return ctx.enter_context(nc.psum_tensor(name, [128, 512], F32))

        def sem(name):
            return ctx.enter_context(nc.semaphore(name))

        q0_parts = nc.dram_tensor("q0_parts", [2, 3, NB // 2, H, S], BF16, kind="Internal").ap()
        k0_parts = nc.dram_tensor("k0_parts", [2, 3, NB // 2, KV0 * D0, S], BF16, kind="Internal").ap()
        q1_parts = nc.dram_tensor("q1_parts", [NB, 3, H, S], BF16, kind="Internal").ap()
        k1_parts = nc.dram_tensor("k1_parts", [NB, 2, 3, H, S], BF16, kind="Internal").ap()
        key_bias_dram = nc.dram_tensor("key_bias_dram", [NB, S], BF16, kind="Internal").ap()

        q_stack = sb("q_stack", [128, 2, NH0 * S], BF16)
        k_stack = sb("k_stack", [128, 2, 2 * NH1 * S], BF16)
        probs = sb("probs", [128, 2, BANKS * 512])
        x_cols = probs[:, 1, 0:HC * T].rearrange("p (c t) -> p c t", c=HC)
        c_cols = probs[:, 1, HC * T:2 * HC * T].rearrange("p (c t) -> p c t", c=HC)
        wq0_sb, wo0_sb = sb("wq0_sb", [128, HC, H]), sb("wo0_sb", [128, HC, H])
        wk0_sb = sb("wk0_sb", [128, HC, KV0 * D0])
        wv_sb = sb("wv_sb", [128, HC, KV0 * D0 + H])
        wq1_sb, wk1_sb, wo1_sb = (sb(n, [128, HC, H]) for n in ("wq1_sb", "wk1_sb", "wo1_sb"))
        w1_sb, w2_sb = sb("w1_sb", [128, HC, F]), sb("w2_sb", [128, FC, H])
        bq0_sb, bq1_sb, bk1_sb = (sb(n, [128, HC]) for n in ("bq0_sb", "bq1_sb", "bk1_sb"))
        bk0_sb, b1_sb = sb("bk0_sb", [KV0 * D0, 1]), sb("b1_sb", [128, FC])
        bv_row = sb("bv_row", [128, KV0 * D0 + H])
        bo0_row, gamma_row, beta_row, bo1_row, post_row, b2_row = (
            sb(n, [128, H]) for n in ("bo0_row", "gamma_row", "beta_row", "bo1_row", "post_row", "b2_row"))
        ident = sb("ident", [128, 128])
        minus_half = sb("minus_half", [128, 1])
        key_mask_sb = sb("key_mask_sb", [NB, S], I32)
        key_bias = sb("key_bias", [NB, S], BF16)
        staged = sb("staged", [128, 2, 512])
        rest = sb("rest", [128, 2, 512])
        part_store = sb("part_store", [128, 2, 3 * 512], BF16)
        parts = part_store[:, :, :].rearrange("c n (p x) -> c n p x", p=3)
        parts_lat = part_store[:, :, 0:3 * H].rearrange("c n (p x) -> c n p x", p=3)
        v_ctx = sb("v_ctx", [128, NB, KV0 * D0 + H])
        v_lat = sb("v_lat", [128, NB, H])
        v0_ones = sb("v0_ones", [128, 2, KV0, 32])
        v1_ones = sb("v1_ones", [128, 2, 2, NH1, 32])
        mask_all = sb("mask_all", [128, NB, S])
        mask_rows = sb("mask_rows", [128, 2, S])
        mask_sb = sb("mask_sb", [128, 2, S])
        resid0 = sb("resid0", [128, NB, H])
        row_max, neg_rest = sb("row_max", [128, NH0]), sb("neg_rest", [128, NH0])
        neg_parts = sb("neg_parts", [128, 3 * NH0], BF16)
        max_cols = sb("max_cols", [3 * NH0, S], BF16)
        ident_bf = sb("ident_bf", [128, 128], BF16)
        o_cols = sb("o_cols", [128, 2, 512])
        inv_sum = sb("inv_sum", [128, 2, 16])
        attn = sb("attn", [128, H])
        attn_cols = sb("attn_cols", [128, HC, S])
        y, y_scaled = sb("y", [128, H]), sb("y_scaled", [128, H])
        stats, mean_var = sb("stats", [128, 6]), sb("mean_var", [128, 2])
        mean_sq, spread, inv_std = sb("mean_sq", [128, 1]), sb("spread", [128, 1]), sb("inv_std", [128, 1])
        normed = sb("normed", [128, 2, H])
        latent_cols = sb("latent_cols", [128, HC, S])
        resid1 = sb("resid1", [128, NB, H])
        resid2 = sb("resid2", [128, NB, H])
        normed_cols = sb("normed_cols", [128, HC, T])
        result = sb("result", [128, 2, H])

        s1_bank = [bank("s1_bank0"), bank("s1_bank1")]
        s2_bank = [bank("s2_bank0"), bank("s2_bank1")]
        pv_bank, ot_bank = bank("pv_bank"), bank("ot_bank")
        m0_bank, m1_bank = bank("m0_bank"), bank("m1_bank")
        job_bank = [s2_bank[0], s2_bank[1], pv_bank, ot_bank]

        ld_wq0, ld_wk0, ld_wk1, ld_wv = (sem(n) for n in ("ld_wq0", "ld_wk0", "ld_wk1", "ld_wv"))
        ld_x = [sem("ld_x0"), sem("ld_x1")]
        ld_c = [sem("ld_c0"), sem("ld_c1")]
        ld_bias, ld_rows, ld_wo0, ld_w1l, ld_mlp, ld_keym = (sem(n) for n in (
            "ld_bias", "ld_rows", "ld_wo0", "ld_w1l", "ld_mlp", "ld_keym"))
        consts, bias_scaled, stacks_init, zeroed = sem("consts"), sem("bias_scaled"), sem("stacks_init"), sem("zeroed")
        key_bias_ready, key_bias_stored = sem("key_bias_ready"), sem("key_bias_stored")
        job_mm, job_staged, job_rest, job_mid, job_split = (sem(n) for n in (
            "job_mm", "job_staged", "job_rest", "job_mid", "job_split"))
        job_stored = [sem("job_stored0"), sem("job_stored1")]
        vctx_mm, vctx_sb, vlat_mm, vlat_sb, v_ready = (sem(n) for n in (
            "vctx_mm", "vctx_sb", "vlat_mm", "vlat_sb", "v_ready"))
        stack_ld = [[sem(f"stack_ld{par}{half}") for half in range(2)] for par in range(2)]
        ld_mask, ld_resid, mask_ready, mask_rows_ready = (sem(n) for n in (
            "ld_mask", "ld_resid", "mask_ready", "mask_rows_ready"))
        resid0_ready = sem("resid0_ready")
        s1_ready, max_ready, neg_ready, neg_rest_ready, neg_mid_ready, max_split, maxT_ready, max_cols_sb = (sem(n) for n in (
            "s1_ready", "max_ready", "neg_ready", "neg_rest_ready", "neg_mid_ready", "max_split", "maxT_ready", "max_cols_sb"))
        max_rows = sem("max_rows")
        s2_ready, p_ready, pv_ready, o_sb, oT_ready, inv_ready, attn_ready = (sem(n) for n in (
            "s2_ready", "p_ready", "pv_ready", "o_sb", "oT_ready", "inv_ready", "attn_ready"))
        attnT_ready, attnT_sb, wo_ready, y_ready, moments, spread_ready, std_ready = (sem(n) for n in (
            "attnT_ready", "attnT_sb", "wo_ready", "y_ready", "moments", "spread_ready", "std_ready"))
        bn_done, scaled_ready, normed_ready, resid12_ready = (sem(n) for n in (
            "bn_done", "scaled_ready", "normed_ready", "resid12_ready"))
        xT_ready, xT_sb = sem("xT_ready"), sem("xT_sb")
        h_mm, h_ready, mlp_mm, result_ready = sem("h_mm"), sem("h_ready"), sem("mlp_mm"), sem("result_ready")
        stored = [sem("stored0"), sem("stored1")]
        passed, stacks_ones = sem("passed"), sem("stacks_ones")
        rows_one, rows_set, query_row_set = sem("rows_one"), sem("rows_set"), sem("query_row_set")

        def iterate(eng, step):
            for i in (-1, 0, 1):
                step(i, i % 2, layers(i))
            with eng.Fori(0, 2) as pair:
                step(pair * 2 + 2, 0, layers(2))
                step(pair * 2 + 3, 1, layers(3))
            for i in (6, 7, 8, 9):
                step(i, i % 2, layers(i))
            with eng.Fori(0, 2) as pair:
                step(pair * 2 + 10, 0, layers(10))
                step(pair * 2 + 11, 1, layers(11))
            for i in (14, 15, 16, 17):
                step(i, i % 2, layers(i))

        def layers(i):
            return [(u // NB if 0 <= u < UNITS else None) for u in (i + 1, i, i - 1, i - 2, i + 2)]

        def need(eng, semaphore, count):
            if not isinstance(count, int) or count > 0:
                eng.wait_ge(semaphore, count)

        def alone(eng):
            eng.sem_inc(passed, 1)

        def at(u, size=1):
            return bass.ds(u, size)

        def stack_need(eng, u, par, layer, half):
            if layer == 0:
                n = (u - par) * (16 * 6 // 2) + 16 * 6
            else:
                n = (u - par - NB) * (16 * 7 // 2) + (16 * 6 * NB // 2 + 16 * 7)
            need(eng, stack_ld[par][half], n)

        block = ctx.enter_context(nc.Block())

        @block.sync
        def _(sp):
            sp.dma_start(wq0_sb[:, :, :], wq0).then_inc(ld_wq0, 16)
            for half in range(2):
                sp.dma_start(x_cols[:, :, half * 512:(half + 1) * 512], xT[:, :, half * 512:(half + 1) * 512]).then_inc(ld_x[half], 16)
                if half == 0:
                    sp.dma_start(bq0_sb[:, :], bq0).then_inc(ld_bias, 16)
                    sp.dma_start(bk0_sb[:, :], bk0).then_inc(ld_bias, 16)
                    sp.dma_start(bq1_sb[:, :], bq1).then_inc(ld_bias, 16)
                    sp.dma_start(bk1_sb[:, :], bk1).then_inc(ld_bias, 16)
                    sp.dma_start(wk0_sb[:, :, :], wk0).then_inc(ld_wk0, 16)
                sp.dma_start(c_cols[:, :, half * 512:(half + 1) * 512], cT[:, :, half * 512:(half + 1) * 512]).then_inc(ld_c[half], 16)
            sp.dma_start(wk1_sb[:, :, :], wk1).then_inc(ld_wk1, 16)
            sp.dma_start(wv_sb[:, :, 0:KV0 * D0], wv0).then_inc(ld_wv, 16)
            sp.dma_start(wv_sb[:, :, KV0 * D0:], wv1).then_inc(ld_wv, 16)

            def store_job(j):
                kind, m, half = JOB[j]
                rows = KV0 * D0 if kind == "k0" else 128
                sp.wait_ge(job_split, j + 1)
                src = parts[0:rows, j % 2, :, :]
                if kind == "k1":
                    for p in range(3):
                        sp.dma_start(k1_parts[4 * half:4 * half + 4, 0, p, m * 128:(m + 1) * 128, :].rearrange("b c t -> c b t"),
                                     src[:, p, :].rearrange("c (b t) -> c b t", b=4)).then_inc(job_stored[j % 2], 16)
                else:
                    dst = k0_parts[half, :, :, :, :] if kind == "k0" else q0_parts[half, :, :, m * 128:(m + 1) * 128, :]
                    sp.dma_start(dst.rearrange("p b c t -> c (p b) t"),
                                 src.rearrange("c p (b t) -> c (p b) t", b=4)).then_inc(job_stored[j % 2], 16)

            def store_latents(b):
                for n in range(2):
                    dst = q1_parts[at(b), :, :, :] if n == 0 else k1_parts[at(b), 1, :, :, :]
                    sp.wait_ge(job_split, b * 2 + (JOBS0 + 1 + n))
                    alone(sp)
                    sp.dma_start(dst.rearrange("o p (m c) t -> c (o p m) t", c=128),
                                 parts_lat[:, n, :, :].rearrange("c p (m t) -> c (p m) t", m=HC)).then_inc(job_stored[n], 16)

            def load_stack(v, par, layer, half):
                need(sp, s2_ready, (v - 2) * BANKS + 4 * (half + 1))
                alone(sp)
                if layer == 0:
                    early = isinstance(v, int) and v < 4
                    sp.wait_ge(job_stored[0], 16 * (2 if early else 3))
                    sp.wait_ge(job_stored[1], 16 * (1 if early else 3))
                    alone(sp)
                    qn, kn = 16 * S, 4 * S
                    which = 0 if early else 1
                    for first, part, n in PAIRS:
                        src = q0_parts[which, part:part + 1, at(v - 4 * which), :, :].rearrange("o c (d h) t -> (o c) d (h t)", d=D0)
                        sp.dma_start(q_stack[first * D0:(first + n) * D0, par, half * qn:(half + 1) * qn],
                                     src[:, :, half * qn:(half + 1) * qn].broadcast_to([n, D0, qn])).then_inc(stack_ld[par][half], 16)
                        src = k0_parts[which, 0:n, at(v - 4 * which), :, :].rearrange("c o (d h) t -> (o c) d (h t)", d=D0)
                        sp.dma_start(k_stack[first * D0:(first + n) * D0, par, half * kn:(half + 1) * kn],
                                     src[:, :, half * kn:(half + 1) * kn]).then_inc(stack_ld[par][half], 16)
                else:
                    b = v - NB
                    sp.wait_ge(rows_set, 2)
                    sp.wait_ge(job_stored[0], b * 16 + (STORED0 + 16))
                    sp.wait_ge(job_stored[1], b * 16 + (STORED0 + 16))
                    alone(sp)
                    first_col = HALF_COL1[half]
                    cols = slice(first_col, first_col + 8 * S)
                    n8 = 8 * S
                    k_halves = k_stack[:, par, :].rearrange("r (c x) -> r c x", c=2)
                    for first, part, n in PAIRS:
                        src = q1_parts[at(b), part:part + 1, :, :].rearrange("o c (d h) t -> (o c) d (h t)", d=D1)
                        sp.dma_start(q_stack[first * D1:(first + n) * D1, par, cols],
                                     src[:, :, half * n8:(half + 1) * n8].broadcast_to([n, D1, n8])).then_inc(stack_ld[par][half], 16)
                        src = k1_parts[at(b), :, 0:n, :, :].rearrange("o a c (d h) t -> (o c) d a (h t)", d=D1)
                        sp.dma_start(k_halves[first * D1:(first + n) * D1, :, cols],
                                     src[:, :, :, half * n8:(half + 1) * n8]).then_inc(stack_ld[par][half], 16)
                    sp.wait_ge(key_bias_stored, 16)
                    sp.dma_start(k_stack[MASK_ROW:MASK_ROW + 1, par, cols],
                                 key_bias_dram[at(b), :].rearrange("o (a s) -> o a s", a=1).broadcast_to([1, 8, S])).then_inc(stack_ld[par][half], 16)

            for j in range(3):
                store_job(j)
            sp.wait_ge(stacks_init, 1)
            load_stack(0, 0, 0, 0)
            sp.dma_start(mask_all[:, :, :], mask.rearrange("b q s -> q b s")).then_inc(ld_mask, 16)
            load_stack(0, 0, 0, 1)
            for j in range(3, 6):
                store_job(j)
            sp.dma_start(key_mask_sb[:, :], key_mask).then_inc(ld_keym, 16)
            sp.dma_start(wo0_sb[:, :, :], wo0).then_inc(ld_wo0, 16)
            sp.dma_start(bv_row[:, 0:KV0 * D0], bv0.broadcast_to([128, KV0 * D0])).then_inc(ld_rows, 16)
            sp.dma_start(bv_row[:, KV0 * D0:], bv1.broadcast_to([128, H])).then_inc(ld_rows, 16)
            for row, src in ((bo0_row, bo0), (gamma_row, gamma), (beta_row, beta), (bo1_row, bo1), (post_row, post_w), (b2_row, b2)):
                sp.dma_start(row[:, :], src.broadcast_to([128, H])).then_inc(ld_rows, 16)
            sp.dma_start(resid0[:, :, :], x.rearrange("b q c -> q b c")).then_inc(ld_resid, 16)
            for j in range(6, JOBS0):
                store_job(j)

            def step(i, par, lay):
                l1, l2, lpv, lpr, lld = lay
                if lld is not None:
                    load_stack(i + 2, par, lld, 0)
                if l1 is not None:
                    sp.wait_ge(max_cols_sb, i + 2)
                    heads = NH1 if l1 else NH0
                    sp.dma_start(q_stack[MAX_ROW:MAX_ROW + 3, 1 - par, 0:heads * S],
                                 max_cols[0:3 * heads, :]).then_inc(max_rows, 16)
                if lld is not None:
                    load_stack(i + 2, par, lld, 1)
                if lpr == 0:
                    store_latents(i - 2)
                if i_is(i, -1):
                    sp.wait_ge(key_bias_ready, 1)
                    sp.dma_start(key_bias_dram, key_bias[:, :]).then_inc(key_bias_stored, 16)
                    sp.dma_start(wq1_sb[:, :, :], wq1).then_inc(ld_w1l, 16)
                    sp.dma_start(wo1_sb[:, :, :], wo1).then_inc(ld_w1l, 16)
                if i_is(i, 0):
                    sp.dma_start(w1_sb[:, :, :], w1).then_inc(ld_mlp, 16)
                    sp.dma_start(b1_sb[:, :], b1).then_inc(ld_mlp, 16)
                    sp.dma_start(w2_sb[:, :, :], w2).then_inc(ld_mlp, 16)

            iterate(sp, step)
            for b in range(NB):
                sp.wait_ge(result_ready, b + 1)
                sp.dma_start(out[b], result[:, b % 2, :]).then_inc(stored[b % 2], 16)
            for par in range(2):
                sp.wait_ge(stored[par], 16 * NB // 2)

        @block.gpsimd
        def _(pool):
            pool.sem_inc(resid12_ready, 3)
            pool.memset(ident[:, :], 0.0).then_inc(zeroed, 1)
            pool.wait_ge(zeroed, 1)
            pool.affine_select(out=ident[:, :], in_=ident[:, :], compare_op=ALU.not_equal, fill=1.0,
                               base=0, pattern=[[-1, 128]], channel_multiplier=1).then_inc(consts, 1)
            pool.wait_ge(consts, 1)
            pool.tensor_copy(ident_bf[:, :], ident[:, :]).then_inc(consts, 1)
            pool.wait_ge(ld_bias, 64)
            pool.tensor_scalar(bq0_sb[:, :], bq0_sb[:, :], SCALE0, None, ALU.mult).then_inc(bias_scaled, 1)
            pool.tensor_scalar(bq1_sb[:, :], bq1_sb[:, :], SCALE1, None, ALU.mult).then_inc(bias_scaled, 1)
            pool.memset(minus_half[:, :], -0.5).then_inc(consts, 1)
            pool.memset(v0_ones[:, :, :, :], 1.0).then_inc(consts, 1)
            pool.memset(v1_ones[:, :, :, :, :], 1.0).then_inc(consts, 1)
            pool.wait_ge(ld_mask, 16)
            pool.tensor_copy(mask_rows[:, 0, :], mask_all[:, 0, :]).then_inc(mask_rows_ready, 1)
            pool.wait_ge(consts, 5)
            pool.wait_ge(ld_rows, 128)

            def step(i, par, lay):
                l1, l2, lpv, lpr, lld = lay
                if lld == 0:
                    need(pool, max_ready, (i + 1) * BANKS)
                    alone(pool)
                    pool.tensor_copy(mask_rows[:, par, :], mask_all[:, at(i + 2), :].rearrange("q o s -> q (o s)")).then_inc(mask_rows_ready, 1)
                if l1 == 0:
                    need(pool, s2_ready, i * BANKS)
                    alone(pool)
                    pool.wait_ge(ld_mask, 16)
                    pool.tensor_copy(mask_sb[:, 1 - par, :], mask_all[:, at(i + 1), :].rearrange("q o s -> q (o s)")).then_inc(mask_ready, 1)
                if i_is(i, -1):
                    pool.wait_ge(ld_resid, 16)
                    for b in range(NB):
                        pool.tensor_tensor(resid0[:, b, :], resid0[:, b, :], bo0_row[:, :], ALU.add).then_inc(resid0_ready, 1)
                if l2 is not None:
                    need(pool, pv_ready, (i - 1) * 2)
                    alone(pool)
                    if l2 == 0:
                        pool.wait_ge(vctx_sb, NB)
                        pool.tensor_copy(v0_ones[:, par, :, 0:D0],
                                         v_ctx[:, at(i), 0:KV0 * D0].rearrange("p o (k d) -> p (o k) d", d=D0)).then_inc(v_ready, 1)
                    else:
                        pool.tensor_copy(v1_ones[:, par, 0, :, 0:D1],
                                         v_ctx[:, at(i - NB), KV0 * D0:].rearrange("p o (k d) -> p (o k) d", d=D1))
                        pool.wait_ge(vlat_sb, i - NB + 1)
                        alone(pool)
                        pool.tensor_copy(v1_ones[:, par, 1, :, 0:D1],
                                         v_lat[:, at(i - NB), :].rearrange("p o (k d) -> p (o k) d", d=D1)).then_inc(v_ready, 1)
                if lpr == 0:
                    pool.wait_ge(normed_ready, i - 1)
                    for resid, row in ((resid1, bo1_row), (resid2, b2_row)):
                        pool.tensor_tensor(resid[:, at(i - 2), :].rearrange("p o c -> p (o c)"), normed[:, par, :],
                                           row[:, :], ALU.add).then_inc(resid12_ready, 1)
                    for n in range(2):
                        j = (i - 2) * 2 + JOBS0 + n
                        pool.wait_ge(job_rest, j + 1)
                        alone(pool)
                        pool.tensor_copy(parts_lat[:, n, 1, :], rest[:, n, 0:H]).then_inc(job_mid, 1)
                        pool.wait_ge(job_mid, j + 1)
                        pool.tensor_tensor(parts_lat[:, n, 2, :], rest[:, n, 0:H], parts_lat[:, n, 1, :], ALU.subtract).then_inc(job_split, 1)
                if lpv is not None:
                    pool.wait_ge(moments, i)
                    alone(pool)
                    if lpv == 0:
                        pool.tensor_scalar(spread[:, :], mean_var[:, 1:2], EPS, None, ALU.add).then_inc(spread_ready, 1)
                    else:
                        pool.tensor_scalar(spread[:, :], mean_sq[:, :], 1.0 / H, EPS, ALU.mult, ALU.add).then_inc(spread_ready, 1)
                    pool.wait_ge(spread_ready, i)
                    pool.tensor_tensor(inv_std[:, :], spread[:, :], minus_half[:, :], ALU.pow).then_inc(std_ready, 1)
            iterate(pool, step)

        @block.tensor
        def _(pe):
            def project(out_ap, w, cols, m, n):
                for c in range(HC):
                    mm = pe.matmul(out_ap, w[:, c, m * 128:m * 128 + n], cols(c), start=(c == 0), stop=(c == HC - 1))
                return mm

            def job(j):
                kind, m, half = JOB[j]
                pe.wait_ge({"q0": ld_wq0, "k0": ld_wk0, "k1": ld_wk1}[kind], 16)
                pe.wait_ge((ld_x if kind == "q0" else ld_c)[half], 16)
                need(pe, job_staged, j - 3)
                w = {"q0": wq0_sb, "k0": wk0_sb, "k1": wk1_sb}[kind]
                src = x_cols if kind == "q0" else c_cols
                rows = KV0 * D0 if kind == "k0" else 128
                project(job_bank[j % 4][0:rows, :], w, lambda c: src[:, c, half * 512:(half + 1) * 512], m, rows).then_inc(job_mm, 1)

            def ctx_values(b):
                if b == 0:
                    pe.wait_ge(ld_wv, 32)
                need(pe, vctx_sb, b - 1)
                for c in range(HC):
                    mm = pe.matmul((m0_bank, m1_bank)[b % 2][:, 0:KV0 * D0 + H], c_cols[:, c, b * S:(b + 1) * S], wv_sb[:, c, :],
                                   start=(c == 0), stop=(c == HC - 1))
                mm.then_inc(vctx_mm, 1)

            def pass1(u, par, layer, k):
                if k % 4 == 0:
                    stack_need(pe, u, par, layer, k // 4)
                need(pe, max_ready, u * BANKS + (k - 1))
                dst = s1_bank[k % 2]
                if layer == 0:
                    for g in range(G0):
                        h = k * G0 + g
                        mm = pe.matmul(dst[:, g * S:(g + 1) * S], q_stack[0:MASK_ROW, par, h * S:(h + 1) * S],
                                       k_stack[0:MASK_ROW, par, k * S:(k + 1) * S], start=True, stop=True)
                else:
                    keys = k_stack[0:MAX_ROW, par, :].rearrange("r (c x) -> r c x", c=2)
                    for g in range(2):
                        col = col1(2 * k + g)
                        mm = pe.matmul(dst[:, g * 2 * S:(g + 1) * 2 * S].rearrange("p (c s) -> p c s", c=2),
                                       q_stack[0:MAX_ROW, par, col:col + S], keys[:, :, col:col + S], start=True, stop=True)
                mm.then_inc(s1_ready, 1)

            def maxima_turned(u, layer, lpr):
                heads = NH1 if layer else NH0
                pe.wait_ge(max_split, u + 1)
                if isinstance(u, int) and u == 0:
                    pe.wait_ge(consts, 2)
                    pe.wait_ge(vctx_sb, NB)
                if lpr == 0:
                    pe.wait_ge(job_staged, (u - 3) * 2 + JOBS0 + 2)
                elif lpr == 1:
                    pe.wait_ge(xT_sb, u - 2)
                else:
                    need(pe, attnT_sb, u - 2)
                pe.matmul(m0_bank[0:3 * heads, 0:S], neg_parts[:, 0:3 * heads], ident_bf[:, :], start=True, stop=True).then_inc(maxT_ready, 1)

            def pass2(u, par, layer, k):
                if k == 0:
                    pe.wait_ge(max_rows, u * 16 + 16)
                    if isinstance(u, int) and u == 0:
                        pe.wait_ge(job_staged, JOBS0)
                        pe.wait_ge(query_row_set, 2)
                need(pe, p_ready, u * BANKS + (k - 1))
                dst = s2_bank[k % 2]
                if layer == 0:
                    if k == 0:
                        pe.wait_ge(mask_ready, u + 1)
                    for g in range(G0):
                        pe.matmul(dst[:, g * S:(g + 1) * S], mask_sb[:, par, :], ident[:, :], is_transpose=True,
                                  start=(g == 0), stop=False)
                    mm = pe.matmul(dst[:, :], k_stack[0:ROWS, par, k * S:(k + 1) * S],
                                   q_stack[0:ROWS, par, k * 512:(k + 1) * 512], start=False, stop=True)
                else:
                    hg, c = k // 2, k % 2
                    for g in range(4):
                        col = col1(4 * hg + g)
                        mm = pe.matmul(dst[:, g * S:(g + 1) * S], k_stack[0:ROWS, par, c * NH1 * S + col:c * NH1 * S + col + S],
                                       q_stack[0:ROWS, par, col:col + S], start=True, stop=True)
                mm.then_inc(s2_ready, 1)

            def values(u, par, layer, half):
                pe.wait_ge(p_ready, u * BANKS + 4 * (half + 1))
                if half == 0:
                    pe.wait_ge(v_ready, u + 1)
                need(pe, o_sb, u * 2 + half)
                if layer == 0:
                    for j in range(4):
                        kv = 4 * half + j
                        mm = pe.matmul(pv_bank[32 * j:32 * j + 32, :], v0_ones[:, par, kv, :], probs[:, par, kv * 512:(kv + 1) * 512],
                                       start=True, stop=True)
                else:
                    for e in range(2):
                        hg = 2 * half + e
                        for c in range(2):
                            for j in range(4):
                                mm = pe.matmul(pv_bank[32 * j:32 * j + 32, e * S:(e + 1) * S], v1_ones[:, par, c, 4 * hg + j, :],
                                               probs[:, par, (2 * hg + c) * 512 + j * S:(2 * hg + c) * 512 + (j + 1) * S],
                                               start=(c == 0), stop=(c == 1))
                mm.then_inc(pv_ready, 1)

            def values_turned(u, layer, half):
                pe.wait_ge(o_sb, u * 2 + half + 1)
                need(pe, attn_ready, u * 2 + half)
                for g in range(2 if layer else 4):
                    mm = pe.transpose(ot_bank[:, g * S:(g + 1) * S], o_cols[:, half, g * S:(g + 1) * S], ident[:, :])
                mm.then_inc(oT_ready, 1)

            def attention_turned(u, more_max):
                pe.wait_ge(attn_ready, u * 2 + 2)
                if more_max:
                    pe.wait_ge(max_cols_sb, u + 3)
                else:
                    need(pe, xT_sb, u)
                for m in range(HC):
                    mm = pe.transpose(m0_bank[:, m * S:(m + 1) * S], attn[:, m * 128:(m + 1) * 128], ident[:, :])
                mm.then_inc(attnT_ready, 1)

            def out_projection(u, layer, lpr):
                pe.wait_ge(attnT_sb, u + 1)
                pe.wait_ge(ld_w1l if layer else ld_wo0, 32 if layer else 16)
                if lpr == 0:
                    pe.wait_ge(vlat_sb, u)
                elif lpr == 1:
                    pe.wait_ge(y_ready, u)
                w = wo1_sb if layer else wo0_sb
                for c in range(HC):
                    mm = pe.matmul(m1_bank[:, 0:H], attn_cols[:, c, :], w[:, c, :], start=(c == 0), stop=(c == HC - 1))
                mm.then_inc(wo_ready, 1)

            def result_turned(u, par):
                pe.wait_ge(normed_ready, u + 1)
                pe.wait_ge(attnT_sb, u + 1)
                for m in range(HC):
                    mm = pe.transpose(m0_bank[:, m * S:(m + 1) * S], normed[:, par, m * 128:(m + 1) * 128], ident[:, :])
                mm.then_inc(xT_ready, 1)

            def latent_queries(b):
                pe.wait_ge(xT_sb, b + 1)
                pe.wait_ge(ld_w1l, 32)
                need(pe, y_ready, b + 1)
                for m in range(HC):
                    mm = project(m1_bank[:, m * S:(m + 1) * S], wq1_sb, lambda c: latent_cols[:, c, :], m, 128)
                mm.then_inc(job_mm, 1)

            def latent_keys(b):
                for m in range(HC):
                    mm = project(m0_bank[:, m * S:(m + 1) * S], wk1_sb, lambda c: latent_cols[:, c, :], m, 128)
                mm.then_inc(job_mm, 1)

            def latent_values(b):
                pe.wait_ge(job_staged, b * 2 + JOBS0 + 1)
                for c in range(HC):
                    mm = pe.matmul(m1_bank[:, 0:H], latent_cols[:, c, :], wv_sb[:, c, KV0 * D0:], start=(c == 0), stop=(c == HC - 1))
                mm.then_inc(vlat_mm, 1)

            pe.sem_inc(xT_ready, 2)
            pe.sem_inc(vlat_mm, 1)
            for j in range(6):
                job(j)

            def step(i, par, lay):
                l1, l2, lpv, lpr, lld = lay
                for k in range(BANKS):
                    if l2 is not None:
                        pass2(i, par, l2, k)
                    if k == 2 and lpr is not None:
                        result_turned(i - 2, par)
                    if k == 3 and lpr == 0:
                        latent_queries(i - 2)
                    if i_is(i, -1):
                        pass1(0, 0, 0, k)
                        if k < JOBS0 - 6:
                            job(6 + k)
                        ctx_values(k)
                    elif l1 is not None and k < 4:
                        pass1(i + 1, 1 - par, l1, 2 * k)
                    if lpv is not None:
                        if k in (0, 2):
                            values(i - 1, 1 - par, lpv, k // 2)
                        if k in (1, 3):
                            values_turned(i - 1, lpv, k // 2)
                    if not i_is(i, -1) and l1 is not None and k < 4:
                        pass1(i + 1, 1 - par, l1, 2 * k + 1)
                    if k == 3 and lpr == 0:
                        latent_keys(i - 2)
                    if k == 4 and lpr == 0:
                        latent_values(i - 2)
                    if k == (7 if i_is(i, -1) else 5) and l1 is not None:
                        maxima_turned(i + 1, l1, lpr)
                    if k == 6 and lpv is not None:
                        attention_turned(i - 1, l1 is not None)
                    if k == 7 and lpv is not None:
                        out_projection(i - 1, lpv, lpr)

            iterate(pe, step)

            pe.wait_ge(ld_mlp, 48)
            pe.wait_ge(xT_sb, UNITS)
            h_bank = [s1_bank[0], s1_bank[1], s2_bank[0], s2_bank[1]]
            for n in range(2 * FC):
                half, m = n // FC, n % FC
                need(pe, h_ready, n - 3)
                if n == 0:
                    pe.wait_ge(max_ready, UNITS * BANKS)
                    pe.wait_ge(p_ready, UNITS * BANKS)
                project(h_bank[n % 4][:, :], w1_sb, lambda c: normed_cols[:, c, half * 512:(half + 1) * 512], m, 128).then_inc(h_mm, 1)
            o_bank = [m0_bank, m1_bank, pv_bank, ot_bank]
            for b in range(NB):
                if b == 0:
                    pe.wait_ge(h_ready, FC)
                    pe.wait_ge(y_ready, UNITS)
                    pe.wait_ge(o_sb, 2 * UNITS)
                    pe.wait_ge(attn_ready, 2 * UNITS)
                if b == NB // 2:
                    pe.wait_ge(h_ready, 2 * FC)
                need(pe, result_ready, b - 3)
                hidden = probs[:, b // 4, :].rearrange("p (m t) -> p m t", m=FC)
                for m in range(FC):
                    mm = pe.matmul(o_bank[b % 4][:, 0:H], hidden[:, m, (b % 4) * S:(b % 4 + 1) * S], w2_sb[:, m, :],
                                   start=(m == 0), stop=(m == FC - 1))
                mm.then_inc(mlp_mm, 1)

        @block.scalar
        def _(act):
            def stage(j):
                kind, m, half = JOB[j]
                rows = KV0 * D0 if kind == "k0" else 128
                if j == 0:
                    act.wait_ge(bias_scaled, 1)
                    act.wait_ge(ld_bias, 64)
                act.wait_ge(job_mm, j + 1)
                need(act, job_split, j - 1)
                need(act, job_stored[j % 2], 16 * min(j // 2, 3) + 48 * max(j // 2 - 3, 0))
                bias = {"q0": bq0_sb[:, m:m + 1], "k0": bk0_sb[:, 0:1], "k1": bk1_sb[:, m:m + 1]}[kind]
                scale = SCALE0 if kind == "q0" else 1.0
                src = job_bank[j % 4][0:rows, :]
                act.activation(staged[0:rows, j % 2, :], src, ACT.Identity, bias=bias, scale=scale)
                act.activation(parts[0:rows, j % 2, 0, :], src, ACT.Identity, bias=bias, scale=scale).then_inc(job_staged, 1)

            def stage_latents(b, n):
                j = b * 2 + (JOBS0 + n)
                act.wait_ge(job_mm, j + 1)
                act.wait_ge(job_split, j - 1)
                act.wait_ge(job_stored[n], b * 16 + STORED0)
                bias, scale = (bq1_sb, SCALE1) if n == 0 else (bk1_sb, 1.0)
                src = (m1_bank, m0_bank)[n]
                for m in range(HC):
                    act.activation(staged[:, n, m * S:(m + 1) * S], src[:, m * S:(m + 1) * S], ACT.Identity,
                                   bias=bias[:, m:m + 1], scale=scale)
                    last = act.activation(parts_lat[:, n, 0, m * S:(m + 1) * S], src[:, m * S:(m + 1) * S], ACT.Identity,
                                          bias=bias[:, m:m + 1], scale=scale)
                last.then_inc(job_staged, 1)

            def maxima_out(u, layer):
                n = 3 * (NH1 if layer else NH0)
                act.wait_ge(maxT_ready, u + 1)
                need(act, max_rows, u * 16)
                act.copy(max_cols[0:n, :], m0_bank[0:n, 0:S]).then_inc(max_cols_sb, 1)

            def exponentials(u, par, k):
                act.wait_ge(s2_ready, u * BANKS + (k + 1))
                if k % 4 == 0:
                    need(act, pv_ready, (u - 2) * 2 + k // 4 + 1)
                act.activation(probs[:, par, k * 512:(k + 1) * 512], s2_bank[k % 2][:, :], ACT.Exp).then_inc(p_ready, 1)

            def values_out(u, layer, half):
                n = 256 if layer else 512
                act.wait_ge(pv_ready, u * 2 + half + 1)
                need(act, oT_ready, u * 2 + (half - 1))
                act.copy(o_cols[:, half, 0:n], pv_bank[:, 0:n]).then_inc(o_sb, 1)

            def attention_out(u):
                act.wait_ge(attnT_ready, u + 1)
                need(act, wo_ready, u)
                act.copy(attn_cols[:, :, :], m0_bank[:, 0:H].rearrange("p (m t) -> p m t", m=HC)).then_inc(attnT_sb, 1)

            def result_out(u, layer):
                act.wait_ge(xT_ready, u + 3)
                src = m0_bank[:, 0:H].rearrange("p (m t) -> p m t", m=HC)
                if layer == 0:
                    need(act, vlat_mm, u + 1)
                    act.copy(latent_cols[:, :, :], src).then_inc(xT_sb, 1)
                else:
                    act.copy(normed_cols[:, :, bass.ds((u - NB) * S, S)], src).then_inc(xT_sb, 1)

            for j in range(6):
                stage(j)
            act.wait_ge(consts, 1)
            act.wait_ge(stacks_init, 1)
            for par in range(2):
                act.activation(q_stack[MASK_ROW:MASK_ROW + 1, par, 0:NH1 * S], ident[96:97, 0:1].broadcast_to([1, NH1 * S]),
                               ACT.Identity, scale=0.0, bias=1.0).then_inc(query_row_set, 1)

            def constant_rows(par):
                n0, n1 = KV0 * S, 2 * NH1 * S
                some = ident[96:128, 0:1]
                act.activation(k_stack[96:128, par, n0:n1], some.broadcast_to([32, n1 - n0]), ACT.Identity,
                               scale=0.0, bias=1.0).then_inc(rows_one, 1)
                act.wait_ge(rows_one, par + 1)
                act.activation(k_stack[MASK_ROW:MASK_ROW + 1, par, n0:n1], some[0:1].broadcast_to([1, n1 - n0]), ACT.Identity,
                               scale=0.0, bias=0.0).then_inc(rows_set, 1)

            def step(i, par, lay):
                l1, l2, lpv, lpr, lld = lay
                if i_is(i, 0) or i_is(i, 1):
                    constant_rows(par)
                for k in range(BANKS):
                    if l2 is not None:
                        exponentials(i, par, k)
                    if i_is(i, -1) and k < JOBS0 - 6:
                        stage(6 + k)
                    if k == 2 and lpr is not None:
                        result_out(i - 2, lpr)
                    if k in (0, 2) and lpv is not None:
                        values_out(i - 1, lpv, k // 2)
                    if k == 3 and lpr == 0:
                        stage_latents(i - 2, 0)
                    if k == 4 and lpr == 0:
                        stage_latents(i - 2, 1)
                    if k == (7 if i_is(i, -1) else 5) and l1 is not None:
                        maxima_out(i + 1, l1)
                    if k == 6 and lpv is not None:
                        attention_out(i - 1)

            iterate(act, step)
            for n in range(2 * FC):
                half, m = n // FC, n % FC
                act.wait_ge(h_mm, n + 1)
                if n == 0:
                    act.wait_ge(pv_ready, 2 * UNITS)
                    act.wait_ge(ld_mlp, 48)
                act.activation(probs[:, half, m * 512:(m + 1) * 512], h_bank_of(n, s1_bank, s2_bank)[:, :], ACT.Gelu_apprx_tanh,
                               bias=b1_sb[:, m:m + 1]).then_inc(h_ready, 1)

        @block.vector
        def _(dve):
            n = KV0 * S
            for par in range(2):
                dve.memset(k_stack[0:96, par, 0:n].bitcast(F32), 0.0)
                last = dve.memset(k_stack[96:128, par, 0:n], 1.0)
            last.then_inc(stacks_ones, 1)
            for par in range(2):
                dve.memset(q_stack[:, par, :].bitcast(F32), 0.0)
            dve.wait_ge(stacks_ones, 1)
            for par in range(2):
                last = dve.memset(k_stack[MASK_ROW:MASK_ROW + 1, par, 0:n].bitcast(F32), 0.0)
            last.then_inc(stacks_init, 1)

            def split(j):
                rows = KV0 * D0 if JOB[j][0] == "k0" else 128
                n = j % 2
                dve.wait_ge(job_staged, j + 1)
                dve.tensor_tensor(rest[0:rows, n, :], staged[0:rows, n, :], parts[0:rows, n, 0, :], ALU.subtract).then_inc(job_rest, 1)
                dve.wait_ge(job_rest, j + 1)
                dve.tensor_copy(parts[0:rows, n, 1, :], rest[0:rows, n, :]).then_inc(job_mid, 1)
                dve.wait_ge(job_mid, j + 1)
                dve.tensor_tensor(parts[0:rows, n, 2, :], rest[0:rows, n, :], parts[0:rows, n, 1, :], ALU.subtract).then_inc(job_split, 1)

            def latent_rest(b, n):
                j = b * 2 + (JOBS0 + n)
                dve.wait_ge(job_staged, j + 1)
                dve.wait_ge(job_split, j - 1)
                dve.tensor_tensor(rest[:, n, 0:H], staged[:, n, 0:H], parts_lat[:, n, 0, :], ALU.subtract).then_inc(job_rest, 1)

            def context_values(b):
                dve.wait_ge(vctx_mm, b + 1)
                if b == 0:
                    dve.wait_ge(ld_rows, 128)
                n = KV0 * D0 + H
                dve.tensor_tensor(v_ctx[:, b, :], (m0_bank, m1_bank)[b % 2][:, 0:n], bv_row[:, :], ALU.add).then_inc(vctx_sb, 1)

            def maxima(u, par, layer, k):
                dve.wait_ge(s1_ready, u * BANKS + (k + 1))
                if k == 0:
                    need(dve, max_split, u)
                    if layer == 0:
                        dve.wait_ge(mask_rows_ready, u + 1)
                if layer == 0:
                    alone(dve)
                    for g in range(G0):
                        h = k * G0 + g
                        last = dve.tensor_tensor_reduce(s1_bank[k % 2][:, g * S:(g + 1) * S], s1_bank[k % 2][:, g * S:(g + 1) * S], mask_rows[:, par, :],
                                                        1.0, LOWEST, ALU.add, ALU.max, row_max[:, h:h + 1])
                    last.then_inc(max_ready, 1)
                else:
                    first = col1(2 * k) // S
                    dve.tensor_reduce(row_max[:, first:first + 2], s1_bank[k % 2][:, :].rearrange("p (h s) -> p h s", h=2),
                                      AX.X, ALU.max).then_inc(max_ready, 1)

            def normalise(u, layer, half):
                dve.wait_ge(oT_ready, u * 2 + half + 1)
                if half == 0:
                    need(dve, attnT_ready, u)
                if layer == 0:
                    turned = ot_bank[:, :].rearrange("q (g j e) -> q j g e", g=G0, j=4)
                    dst = attn[:, half * 128:(half + 1) * 128].rearrange("q (j g d) -> q j g d", j=4, g=G0)
                    d, n = D0, 16
                    inv = inv_sum[:, half, 0:16].rearrange("q (j g a) -> q j g a", j=4, g=G0)
                    shape = [128, 4, G0, D0]
                else:
                    turned = ot_bank[:, 0:2 * S].rearrange("q (e j c) -> q e j c", e=2, j=4)
                    dst = attn[:, half * 128:(half + 1) * 128].rearrange("q (e j d) -> q e j d", e=2, j=4)
                    d, n = D1, 8
                    inv = inv_sum[:, half, 0:8].rearrange("q (e j a) -> q e j a", e=2, j=4)
                    shape = [128, 2, 4, D1]
                dve.reciprocal(inv, turned[:, :, :, d:d + 1]).then_inc(inv_ready, 1)
                dve.wait_ge(inv_ready, u * 2 + half + 1)
                dve.tensor_tensor(dst, turned[:, :, :, 0:d], inv.broadcast_to(shape), ALU.mult).then_inc(attn_ready, 1)

            def residual_sum(u, par, layer):
                dve.wait_ge(wo_ready, u + 1)
                need(dve, normed_ready, u)
                if layer == 0:
                    dve.wait_ge(resid0_ready, NB)
                    dve.tensor_tensor(y[:, :], m1_bank[:, 0:H], resid0[:, at(u), :].rearrange("q o c -> q (o c)"), ALU.add).then_inc(y_ready, 1)
                    dve.wait_ge(y_ready, u + 1)
                    dve.bn_stats(stats[:, :], y[:, :]).then_inc(bn_done, 1)
                    dve.wait_ge(bn_done, u + 1)
                    alone(dve)
                    dve.bn_aggr(mean_var[:, :], stats[:, :]).then_inc(moments, 1)
                else:
                    dve.wait_ge(resid12_ready, 2 * NB + 3)
                    dve.tensor_tensor(y[:, :], m1_bank[:, 0:H], resid1[:, at(u - NB), :].rearrange("p o c -> p (o c)"), ALU.add).then_inc(y_ready, 1)
                    dve.wait_ge(y_ready, u + 1)
                    dve.tensor_tensor_reduce(y_scaled[:, :], y[:, :], y[:, :], 1.0, 0.0, ALU.mult, ALU.add, mean_sq[:, :]).then_inc(moments, 1)

            def split_maxima(u, layer):
                heads = NH1 if layer else NH0
                maxima_of_unit, rest_of_max = row_max[:, 0:heads], neg_rest[:, 0:heads]
                part = [neg_parts[:, p * heads:(p + 1) * heads] for p in range(3)]
                dve.wait_ge(max_ready, u * BANKS + BANKS)
                need(dve, maxT_ready, u)
                dve.tensor_scalar(part[0], maxima_of_unit, -1.0, None, ALU.mult).then_inc(neg_ready, 1)
                dve.wait_ge(neg_ready, u + 1)
                dve.scalar_tensor_tensor(rest_of_max, maxima_of_unit, -1.0, part[0], ALU.mult, ALU.subtract).then_inc(neg_rest_ready, 1)
                dve.wait_ge(neg_rest_ready, u + 1)
                dve.tensor_copy(part[1], rest_of_max).then_inc(neg_mid_ready, 1)
                dve.wait_ge(neg_mid_ready, u + 1)
                dve.tensor_tensor(part[2], rest_of_max, part[1], ALU.subtract).then_inc(max_split, 1)

            def norm(u, par, layer):
                dve.wait_ge(std_ready, u + 1)
                dve.wait_ge(xT_ready, u + 1)
                if layer == 0:
                    dve.wait_ge(resid12_ready, u * 2 + 1)
                    dve.scalar_tensor_tensor(y_scaled[:, :], y[:, :], mean_var[:, 0:1], gamma_row[:, :], ALU.subtract, ALU.mult).then_inc(scaled_ready, 1)
                    dve.wait_ge(scaled_ready, u + 1)
                    dve.scalar_tensor_tensor(normed[:, par, :], y_scaled[:, :], inv_std[:, 0:1], beta_row[:, :], ALU.mult, ALU.add).then_inc(normed_ready, 1)
                else:
                    dve.scalar_tensor_tensor(normed[:, par, :], y[:, :], inv_std[:, 0:1], post_row[:, :], ALU.mult, ALU.mult).then_inc(normed_ready, 1)

            for j in range(6):
                split(j)

            def step(i, par, lay):
                l1, l2, lpv, lpr, lld = lay
                for k in range(BANKS):
                    if i_is(i, -1):
                        maxima(0, 0, 0, k)
                        if k < JOBS0 - 6:
                            split(6 + k)
                        context_values(k)
                    elif l1 is not None and k < 4:
                        maxima(i + 1, 1 - par, l1, 2 * k)
                        maxima(i + 1, 1 - par, l1, 2 * k + 1)
                    if k == 0 and lpr is not None:
                        norm(i - 2, par, lpr)
                    if k == (7 if i_is(i, -1) else 3) and l1 is not None:
                        split_maxima(i + 1, l1)
                    if k in (1, 3) and lpv is not None:
                        normalise(i - 1, lpv, k // 2)
                    if k == 4 and lpr == 0:
                        latent_rest(i - 2, 0)
                        latent_rest(i - 2, 1)
                    if k == 5 and lpr == 0:
                        dve.wait_ge(vlat_mm, i)
                        dve.tensor_tensor(v_lat[:, at(i - 2), :].rearrange("p o c -> p (o c)"), m1_bank[:, 0:H],
                                          bv_row[:, KV0 * D0:], ALU.add).then_inc(vlat_sb, 1)
                    if k == 7 and lpv is not None:
                        residual_sum(i - 1, 1 - par, lpv)
                if i_is(i, -1):
                    dve.wait_ge(ld_keym, 16)
                    dve.tensor_scalar(key_bias[:, :], key_mask_sb[:, :], 0.0, MASKED, ALU.is_equal, ALU.mult).then_inc(key_bias_ready, 1)

            iterate(dve, step)
            for b in range(NB):
                dve.wait_ge(mlp_mm, b + 1)
                need(dve, stored[b % 2], 16 * (b // 2))
                dve.tensor_tensor(result[:, b % 2, :], [m0_bank, m1_bank, pv_bank, ot_bank][b % 4][:, 0:H], resid2[:, b, :], ALU.add).then_inc(result_ready, 1)


JOB = [(kind, m, half) for half in range(2) for kind, m in (("q0", 0), ("q0", 1), ("k0", 0))]
JOB += [("k1", m, half) for half in range(2) for m in range(2)]


def col1(h):
    return HALF_COL1[h // 8] + (h % 8) * S


def i_is(i, n):
    return isinstance(i, int) and i == n


def h_bank_of(n, s1_bank, s2_bank):
    return [s1_bank[0], s1_bank[1], s2_bank[0], s2_bank[1]][n % 4]


def kernel(**inputs):
    import numpy as np
    import concourse.bacc as bacc
    from concourse.bass_utils import run_bass_kernel_spmd

    a = {k: np.asarray(v) for k, v in inputs.items()}

    def cols(w):
        return np.ascontiguousarray(w.reshape(-1, 128, w.shape[1]).transpose(1, 0, 2))

    def tokens(v):
        return cols(v.reshape(T, H).T)

    def d_major(w, heads, d):
        return w.reshape(-1, heads, d).transpose(0, 2, 1).reshape(-1, heads * d)

    kv_w = a["L1_xattn_kv_w"].reshape(H, NH1, D1, 2)
    kv_b = a["L1_xattn_kv_b"].reshape(1, NH1, D1, 2)

    def column(v):
        return cols(v.reshape(-1, 1))[:, :, 0]

    arrays = {
        "xT": tokens(a["x"]), "x": a["x"], "cT": tokens(a["ctx_2048"]),
        "mask": a["mask_Bx1xSxS2_ff0"].reshape(NB, S, S), "key_mask": a["mask_BxS2_ik0"],
        "wq0": cols(d_major(a["L0_xattn_Wq"], NH0, D0)), "bq0": column(d_major(a["L0_xattn_bq"], NH0, D0)),
        "wk0": cols(d_major(a["L0_xattn_Wk"], KV0, D0)), "bk0": d_major(a["L0_xattn_bk"], KV0, D0).reshape(-1, 1),
        "wv0": cols(a["L0_xattn_Wv"]), "bv0": a["L0_xattn_bv"].reshape(1, -1),
        "wo0": cols(a["L0_xattn_Wo"]), "bo0": a["L0_xattn_bo"].reshape(1, -1),
        "gamma": a["L0_xattn_gamma"].reshape(1, -1), "beta": a["L0_xattn_beta"].reshape(1, -1),
        "wq1": cols(d_major(a["L1_xattn_q_w"], NH1, D1)), "bq1": column(d_major(a["L1_xattn_q_b"], NH1, D1)),
        "wk1": cols(d_major(kv_w[..., 0].reshape(H, H), NH1, D1)), "bk1": column(d_major(kv_b[..., 0].reshape(1, H), NH1, D1)),
        "wv1": cols(kv_w[..., 1].reshape(H, H)), "bv1": kv_b[..., 1].reshape(1, H),
        "wo1": cols(a["L1_xattn_out_w"]), "bo1": a["L1_xattn_out_b"].reshape(1, -1),
        "post_w": a["L1_xattn_postnorm_w"].reshape(1, -1),
        "w1": cols(a["L1_xattn_mlp_w1"]), "b1": column(a["L1_xattn_mlp_b1"]),
        "w2": cols(a["L1_xattn_mlp_w2"]), "b2": a["L1_xattn_mlp_b2"].reshape(1, -1),
    }
    nc = bacc.Bacc("TRN2", target_bir_lowering=False, num_devices=1)
    args, feed = [], {}
    for name, v in arrays.items():
        v = np.ascontiguousarray(v)
        feed[f"in_{name}"] = v
        args.append(nc.dram_tensor(f"in_{name}", v.shape, mybir.dt.from_np(v.dtype), kind="ExternalInput").ap())
    out = nc.dram_tensor("out_0", (NB, S, H), F32, kind="ExternalOutput").ap()
    cross_attention_layers(nc, *args, out)
    r = run_bass_kernel_spmd(nc, [feed], core_ids=[0])
    return r.results[0]["out_0"]
```

```python
from contextlib import ExitStack

import concourse.bass as bass
from concourse import mybir

F32 = mybir.dt.float32
BF16 = mybir.dt.bfloat16
I32 = mybir.dt.int32
ALU = mybir.AluOpType
ACT = mybir.ActivationFunctionType
AX = mybir.AxisListType

NB, S, H = 8, 128, 256
T = NB * S
HC = H // 128
NH0, KV0, D0 = 32, 8, 8
G0 = NH0 // KV0
NH1, D1 = 16, 16
F = 4 * H
FC = F // 128
BIAS_VALUES = HC + 1 + HC + HC + FC
BV_VALUES = KV0 * D0 + H
ROW_VALUES = BV_VALUES + 6 * H
SCALE0 = float(D0) ** -0.5
SCALE1 = 1.0 / D1
EPS = 1e-6
BANKS = 8
LOWEST = -3.0e38
MASKED = -1.0e30
UNITS = 2 * NB
MASK_ROW, MAX_ROW, ROWS = 96, 97, 100
HALF_COL1 = (8 * S, 0)
PAIRS = ((0, 0, 3), (3, 1, 2), (5, 2, 1))
JOB = [(kind, m, b, n) for b, n in ((0, 1), (1, 3), (4, 4)) for kind, m in (("q0", 0), ("q0", 1), ("k0", 0))]
JOB += [("k1", m, b, 4) for b in (0, 4) for m in range(2)]
JOBS0 = len(JOB)
JOBS_L0 = 9
JOB_BUFS = 3
PV_SLOTS, TURN_SLOTS = ((0, 2), (0, 3)), ((1, 3), (1, 5))
LEAD = 1
HIDDEN_AT = {(16, 0): (0,), (16, 2): (1,), (16, 3): (2,), (16, 6): (3,), (16, 7): (4,), (17, 0): (5, 6), (17, 7): (7,)}
QUERY_BLOCKS, KEY_BLOCKS = (0, 1, 2, 0, 1, 0), (2, 1, 0, 1, 0, 0)
BLOCKS = len(KEY_BLOCKS)
QUERY_RUNS, KEY_RUNS = ((0, 3, 0), (3, 2, 0), (5, 1, 0)), ((0, 3, 0), (3, 2, 1), (5, 1, 2))


def cross_attention_layers(nc, xT, x, cT, mask, key_mask, biases, rows, wq0, wk0, wv, wo0, wq1, wk1, wo1, w1, w2, out):
    ctx = ExitStack()
    with ctx:
        def sb(name, shape, dt=F32):
            return ctx.enter_context(nc.sbuf_tensor(name, shape, dt))

        def bank(name):
            return ctx.enter_context(nc.psum_tensor(name, [128, 512], F32))

        def sem(name):
            return ctx.enter_context(nc.semaphore(name))

        q0_parts = nc.dram_tensor("q0_parts", [NB, 3, H, S], BF16, kind="Internal").ap()
        k0_parts = nc.dram_tensor("k0_parts", [NB, 3, KV0 * D0, S], BF16, kind="Internal").ap()
        q1_parts = nc.dram_tensor("q1_parts", [NB, BLOCKS, H, S], BF16, kind="Internal").ap()
        k1_parts = nc.dram_tensor("k1_parts", [2, NB, BLOCKS, H, S], BF16, kind="Internal").ap()
        key_bias_dram = nc.dram_tensor("key_bias_dram", [NB, S], BF16, kind="Internal").ap()

        q_stack = sb("q_stack", [128, 2, NH0 * S], BF16)
        k_stack = sb("k_stack", [128, 2, 2 * NH1 * S], BF16)
        probs = sb("probs", [128, 2, BANKS * 512])
        x_cols = probs[:, 1, 0:HC * T].rearrange("p (c t) -> p c t", c=HC)
        c_cols = probs[:, 1, HC * T:2 * HC * T].rearrange("p (c t) -> p c t", c=HC)
        wq0_sb, wo0_sb = sb("wq0_sb", [128, HC, H]), sb("wo0_sb", [128, HC, H])
        wk0_sb = sb("wk0_sb", [128, HC, KV0 * D0])
        wv_sb = sb("wv_sb", [128, HC, KV0 * D0 + H])
        wq1_sb, wk1_sb, wo1_sb = (sb(n, [128, HC, H]) for n in ("wq1_sb", "wk1_sb", "wo1_sb"))
        w1_sb, w2_sb = sb("w1_sb", [128, HC, F]), sb("w2_sb", [128, FC, H])
        biases_sb = sb("biases_sb", [128, BIAS_VALUES])
        bq0_sb, bk0_sb, bq1_sb, bk1_sb, b1_sb = pieces(biases_sb, (HC, 1, HC, HC, FC))
        rows_sb = sb("rows_sb", [128, ROW_VALUES])
        bv_row, bo0_row, gamma_row, beta_row, bo1_row, post_row, b2_row = pieces(rows_sb, (BV_VALUES,) + 6 * (H,))
        ident = sb("ident", [128, 128])
        minus_half = sb("minus_half", [128, 1])
        key_mask_sb = sb("key_mask_sb", [NB, S], I32)
        key_bias = sb("key_bias", [NB, S], BF16)
        staged = sb("staged", [128, JOB_BUFS, 512])
        rest = sb("rest", [128, JOB_BUFS, 512])
        part_store = sb("part_store", [128, JOB_BUFS, 4 * 3 * S], BF16)
        staged_lat, rest_lat = staged[:, 1:3, 0:H], rest[:, 1:3, 0:H]
        parts_lat = part_store[:, 1:3, 0:3 * H].rearrange("c n (p x) -> c n p x", p=3)
        lat_part = [[parts_lat[:, 0, p, :] for p in range(3)], [parts_lat[:, 1, 2 - p, :] for p in range(3)]]
        v_ctx = sb("v_ctx", [128, NB, KV0 * D0 + H])
        v_lat = sb("v_lat", [128, NB, H])
        v0_ones = sb("v0_ones", [128, 2, KV0, 32])
        v1_ones = sb("v1_ones", [128, 2, 2, NH1, 32])
        mask_all = sb("mask_all", [128, NB, S])
        mask_rows = sb("mask_rows", [128, 2, S])
        mask_sb = sb("mask_sb", [128, 2, S])
        resid0 = sb("resid0", [128, NB, H])
        row_max, neg_rest = sb("row_max", [128, NH0]), sb("neg_rest", [128, NH0])
        neg_parts = sb("neg_parts", [128, 3 * NH0], BF16)
        max_cols = sb("max_cols", [3 * NH0, S], BF16)
        ident_bf = sb("ident_bf", [128, 128], BF16)
        o_cols = sb("o_cols", [128, 2, 512])
        inv_sum = sb("inv_sum", [128, 2, 16])
        attn = sb("attn", [128, H])
        attn_cols = sb("attn_cols", [128, HC, S])
        y, y_scaled = sb("y", [128, H]), sb("y_scaled", [128, H])
        stats, mean_var = sb("stats", [128, 6]), sb("mean_var", [128, 2])
        mean_sq, spread, inv_std = sb("mean_sq", [128, 1]), sb("spread", [128, 1]), sb("inv_std", [128, 1])
        normed = sb("normed", [128, 2, H])
        latent_cols = sb("latent_cols", [128, HC, S])
        resid1 = sb("resid1", [128, NB, H])
        resid2 = sb("resid2", [128, NB, H])
        normed_cols = sb("normed_cols", [128, HC, T])
        result = sb("result", [128, 2, H])

        s1_bank = [bank("s1_bank0"), bank("s1_bank1")]
        s2_bank = [bank("s2_bank0"), bank("s2_bank1")]
        pv_bank, ot_bank = bank("pv_bank"), bank("ot_bank")
        m0_bank, m1_bank = bank("m0_bank"), bank("m1_bank")
        h_bank, o_bank = s1_bank + s2_bank, [m0_bank, m1_bank, pv_bank, ot_bank]
        job_bank = [ot_bank, s2_bank[0], s2_bank[1], pv_bank]

        ld_wq0, ld_wk0, ld_wk1, ld_wv = (sem(n) for n in ("ld_wq0", "ld_wk0", "ld_wk1", "ld_wv"))
        ld_x = {0: sem("ld_x0"), 1: sem("ld_x1"), 4: sem("ld_x4")}
        ld_c = {0: sem("ld_c0"), 1: sem("ld_c1"), 4: sem("ld_c4")}
        ld_bias, ld_bv, ld_rows, ld_wo0, ld_w1l, ld_mlp, ld_keym = (sem(n) for n in (
            "ld_bias", "ld_bv", "ld_rows", "ld_wo0", "ld_w1l", "ld_mlp", "ld_keym"))
        consts, bias_scaled, stacks_init, zeroed = sem("consts"), sem("bias_scaled"), sem("stacks_init"), sem("zeroed")
        key_bias_ready, key_bias_stored = sem("key_bias_ready"), sem("key_bias_stored")
        job_mm, job_staged, job_rest, job_mid, job_split = (sem(n) for n in (
            "job_mm", "job_staged", "job_rest", "job_mid", "job_split"))
        job_stored = [sem(f"job_stored{n}") for n in range(JOB_BUFS)]
        vctx_mm, vctx_sb, vlat_mm, vlat_sb, v_ready = (sem(n) for n in (
            "vctx_mm", "vctx_sb", "vlat_mm", "vlat_sb", "v_ready"))
        stack_ld = [[sem(f"stack_ld{par}{half}") for half in range(2)] for par in range(2)]
        ld_mask, ld_resid, mask_ready, mask_rows_ready = (sem(n) for n in (
            "ld_mask", "ld_resid", "mask_ready", "mask_rows_ready"))
        resid0_ready = sem("resid0_ready")
        s1_ready, max_ready, neg_ready, neg_rest_ready, neg_mid_ready, max_split, maxT_ready, max_cols_sb = (sem(n) for n in (
            "s1_ready", "max_ready", "neg_ready", "neg_rest_ready", "neg_mid_ready", "max_split", "maxT_ready", "max_cols_sb"))
        max_rows = sem("max_rows")
        s2_ready, p_ready, pv_ready, o_sb, oT_ready, inv_ready, attn_ready = (sem(n) for n in (
            "s2_ready", "p_ready", "pv_ready", "o_sb", "oT_ready", "inv_ready", "attn_ready"))
        attnT_ready, attnT_sb, wo_ready, y_ready, moments, spread_ready, std_ready = (sem(n) for n in (
            "attnT_ready", "attnT_sb", "wo_ready", "y_ready", "moments", "spread_ready", "std_ready"))
        bn_done, scaled_ready, normed_ready, resid12_ready = (sem(n) for n in (
            "bn_done", "scaled_ready", "normed_ready", "resid12_ready"))
        xT_ready, xT_sb = sem("xT_ready"), sem("xT_sb")
        h_mm, h_ready, mlp_mm, result_ready = sem("h_mm"), sem("h_ready"), sem("mlp_mm"), sem("result_ready")
        stored = [sem("stored0"), sem("stored1")]
        passed, stacks_ones = sem("passed"), sem("stacks_ones")
        rows_one, rows_set, query_row_set = sem("rows_one"), sem("rows_set"), sem("query_row_set")

        def iterate(eng, step):
            for i in (-1, 0, 1):
                step(i, i % 2, layers(i))
            with eng.Fori(0, 2) as pair:
                step(pair * 2 + 2, 0, layers(2))
                step(pair * 2 + 3, 1, layers(3))
            for i in (6, 7, 8, 9):
                step(i, i % 2, layers(i))
            with eng.Fori(0, 2) as pair:
                step(pair * 2 + 10, 0, layers(10))
                step(pair * 2 + 11, 1, layers(11))
            for i in (14, 15, 16, 17):
                step(i, i % 2, layers(i))

        def layers(i):
            return [(u // NB if 0 <= u < UNITS else None) for u in (i + 1, i, i - 1, i - 2, i + 2)]

        def need(eng, semaphore, count):
            if not isinstance(count, int) or count > 0:
                eng.wait_ge(semaphore, count)

        def alone(eng):
            eng.sem_inc(passed, 1)

        stored_jobs = [stored_before(JOBS0 + (n - JOBS0) % JOB_BUFS) for n in range(JOB_BUFS)]

        def job_views(j):
            kind, m, b, n = JOB[j]
            rows = KV0 * D0 if kind == "k0" else 128
            whole = [t[0:rows, j % JOB_BUFS, 0:n * S].rearrange("c (b t) -> c b t", b=n) for t in (staged, rest)]
            part = part_store[0:rows, j % JOB_BUFS, 0:n * 3 * S].rearrange("c (b p t) -> c b p t", b=n, p=3)
            return whole[0], whole[1], [part[:, :, p, :] for p in range(3)]

        def at(u, size=1):
            return bass.ds(u, size)

        def stack_need(eng, u, par, layer, half):
            if layer == 0:
                n = (u - par) * (16 * 6 // 2) + 16 * 6
            else:
                n = (u - par - NB) * (16 * 3 // 2) + (16 * 6 * NB // 2 + 16 * 3)
            need(eng, stack_ld[par][half], n)

        block = ctx.enter_context(nc.Block())

        @block.sync
        def _(sp):
            def load_columns(b, n):
                cols = slice(b * S, (b + n) * S)
                sp.dma_start(x_cols[:, :, cols], xT[:, :, cols]).then_inc(ld_x[b], 16)
                if b == 0:
                    sp.dma_start(wq0_sb[:, :, :], wq0).then_inc(ld_wq0, 16)
                sp.dma_start(c_cols[:, :, cols], cT[:, :, cols]).then_inc(ld_c[b], 16)

            sp.dma_start(biases_sb[:, :], biases).then_inc(ld_bias, 16)
            load_columns(0, 1)
            sp.dma_start(wk0_sb[:, :, :], wk0).then_inc(ld_wk0, 16)
            load_columns(1, 3)
            load_columns(4, 4)
            sp.dma_start(wv_sb[:, :, :], wv).then_inc(ld_wv, 16)
            sp.dma_start(wk1_sb[:, :, :], wk1).then_inc(ld_wk1, 16)
            sp.dma_start(bv_row, rows[:, 0:BV_VALUES].broadcast_to([128, BV_VALUES])).then_inc(ld_bv, 16)

            def store_job(j):
                kind, m, b, n = JOB[j]
                rows = KV0 * D0 if kind == "k0" else 128
                sp.wait_ge(job_split, j + 1)
                if kind == "k1":
                    for block, p in enumerate(KEY_BLOCKS):
                        sp.dma_start(k1_parts[0, b:b + n, block, m * 128:(m + 1) * 128, :].rearrange("b c t -> c b t"),
                                     job_views(j)[2][p]).then_inc(job_stored[j % JOB_BUFS], 16)
                    return
                dst = q0_parts if kind == "q0" else k0_parts
                sp.dma_start(dst[b:b + n, :, m * 128:m * 128 + rows, :].rearrange("b p c t -> c (b p) t"),
                             part_store[0:rows, j % JOB_BUFS, 0:n * 3 * S].rearrange("c (x t) -> c x t", t=S)).then_inc(job_stored[j % JOB_BUFS], 16)

            def store_latents(b):
                for n in range(2):
                    dst = q1_parts[at(b), :, :, :] if n == 0 else k1_parts[1, at(b), :, :, :]
                    sp.wait_ge(job_split, b * 2 + (JOBS0 + 1 + n))
                    alone(sp)
                    for first, count, place in (QUERY_RUNS, KEY_RUNS)[n]:
                        sp.dma_start(dst[:, first:first + count, :, :].rearrange("o p (m c) t -> c (o p m) t", c=128),
                                     parts_lat[:, n, place:place + count, :].rearrange("c p (m t) -> c (p m) t", m=HC)).then_inc(job_stored[n + 1], 16)

            def load_stack(v, par, layer, half):
                need(sp, s2_ready, (v - 2) * BANKS + 4 * (half + 1))
                alone(sp)
                if layer == 0:
                    done = (1 if v == 0 else 2 if v < 4 else 3) if isinstance(v, int) else 3
                    for n in range(JOB_BUFS):
                        sp.wait_ge(job_stored[n], 16 * done)
                    alone(sp)
                    qn, kn = 16 * S, 4 * S
                    for first, part, n in PAIRS:
                        src = q0_parts[at(v), part:part + 1, :, :].rearrange("o c (d h) t -> (o c) d (h t)", d=D0)
                        sp.dma_start(q_stack[first * D0:(first + n) * D0, par, half * qn:(half + 1) * qn],
                                     src[:, :, half * qn:(half + 1) * qn].broadcast_to([n, D0, qn])).then_inc(stack_ld[par][half], 16)
                        src = k0_parts[at(v), 0:n, :, :].rearrange("o c (d h) t -> (o c) d (h t)", d=D0)
                        sp.dma_start(k_stack[first * D0:(first + n) * D0, par, half * kn:(half + 1) * kn],
                                     src[:, :, half * kn:(half + 1) * kn]).then_inc(stack_ld[par][half], 16)
                else:
                    b = v - NB
                    sp.wait_ge(rows_set, 2)
                    sp.wait_ge(job_stored[0], stored_jobs[0])
                    sp.wait_ge(job_stored[1], b * 48 + (stored_jobs[1] + 48))
                    sp.wait_ge(job_stored[2], b * 48 + (stored_jobs[2] + 48))
                    alone(sp)
                    first_col = HALF_COL1[half]
                    cols = slice(first_col, first_col + 8 * S)
                    n8 = 8 * S
                    k_halves = k_stack[:, par, :].rearrange("r (c x) -> r c x", c=2)
                    src = q1_parts[at(b), :, :, :].rearrange("o p (d h) t -> (o p d) (h t)", d=D1)
                    sp.dma_start(q_stack[0:BLOCKS * D1, par, cols], src[:, half * n8:(half + 1) * n8]).then_inc(stack_ld[par][half], 16)
                    src = k1_parts[:, at(b), :, :, :].rearrange("a o p (d h) t -> (o p d) a (h t)", d=D1)
                    sp.dma_start(k_halves[0:BLOCKS * D1, :, cols], src[:, :, half * n8:(half + 1) * n8]).then_inc(stack_ld[par][half], 16)
                    sp.wait_ge(key_bias_stored, 16)
                    sp.dma_start(k_stack[MASK_ROW:MASK_ROW + 1, par, cols],
                                 key_bias_dram[at(b), :].rearrange("o (a s) -> o a s", a=1).broadcast_to([1, 8, S])).then_inc(stack_ld[par][half], 16)

            for j in range(3):
                store_job(j)
            sp.wait_ge(stacks_init, 1)
            load_stack(0, 0, 0, 0)
            sp.dma_start(mask_all[:, :, :], mask.rearrange("b q s -> q b s")).then_inc(ld_mask, 16)
            for j in range(3, 5):
                store_job(j)
            load_stack(0, 0, 0, 1)
            store_job(5)
            sp.dma_start(key_mask_sb[:, :], key_mask).then_inc(ld_keym, 16)
            sp.wait_ge(stacks_init, 2)
            for half in range(2):
                load_stack(1, 1, 0, half)
            for j in range(6, JOBS_L0):
                store_job(j)

            def step(i, par, lay):
                l1, l2, lpv, lpr, lld = lay
                if lld is not None and not i_is(i, -1):
                    load_stack(i + 2, par, lld, 0)
                if l1 is not None:
                    if i_is(i, -1):
                        sp.wait_ge(query_row_set, 2)
                    sp.wait_ge(max_cols_sb, i + 2)
                    heads = NH1 if l1 else NH0
                    sp.dma_start(q_stack[MAX_ROW:MAX_ROW + 3, 1 - par, 0:heads * S],
                                 max_cols[0:3 * heads, :]).then_inc(max_rows, 16)
                if lld is not None and not i_is(i, -1):
                    load_stack(i + 2, par, lld, 1)
                if lpr == 0:
                    store_latents(i - 2)
                if i_is(i, UNITS - 2):
                    sp.dma_start(w1_sb[:, :, :], w1).then_inc(ld_mlp, 16)
                    sp.dma_start(w2_sb[:, :, :], w2).then_inc(ld_mlp, 16)
                if i_is(i, 1):
                    for j in range(JOBS_L0 + 2, JOBS0):
                        store_job(j)
                if i_is(i, -1):
                    sp.dma_start(resid0[:, :, :], x.rearrange("b q c -> q b c")).then_inc(ld_resid, 16)
                    sp.dma_start(rows_sb[:, BV_VALUES:], rows[:, BV_VALUES:].broadcast_to([128, ROW_VALUES - BV_VALUES])).then_inc(ld_rows, 16)
                    store_job(JOBS_L0)
                    sp.wait_ge(key_bias_ready, 1)
                    sp.dma_start(key_bias_dram, key_bias[:, :]).then_inc(key_bias_stored, 16)
                    sp.dma_start(wq1_sb[:, :, :], wq1).then_inc(ld_w1l, 16)
                    sp.dma_start(wo1_sb[:, :, :], wo1).then_inc(ld_w1l, 16)
                if i_is(i, 0):
                    sp.dma_start(wo0_sb[:, :, :], wo0).then_inc(ld_wo0, 16)
                    store_job(JOBS_L0 + 1)

            iterate(sp, step)
            for b in range(NB):
                sp.wait_ge(result_ready, b + 1)
                sp.dma_start(out[b], result[:, b % 2, :]).then_inc(stored[b % 2], 16)
            for par in range(2):
                sp.wait_ge(stored[par], 16 * NB // 2)

        @block.gpsimd
        def _(pool):
            pool.sem_inc(resid12_ready, 3)
            pool.memset(ident[:, :], 0.0).then_inc(zeroed, 1)
            pool.wait_ge(zeroed, 1)
            pool.affine_select(out=ident[:, :], in_=ident[:, :], compare_op=ALU.not_equal, fill=1.0,
                               base=0, pattern=[[-1, 128]], channel_multiplier=1).then_inc(consts, 1)
            pool.wait_ge(consts, 1)
            pool.tensor_copy(ident_bf[:, :], ident[:, :]).then_inc(consts, 1)
            pool.wait_ge(ld_bias, 16)
            pool.tensor_scalar(bq0_sb, bq0_sb, SCALE0, None, ALU.mult).then_inc(bias_scaled, 1)
            pool.tensor_scalar(bq1_sb, bq1_sb, SCALE1, None, ALU.mult).then_inc(bias_scaled, 1)
            pool.memset(minus_half[:, :], -0.5).then_inc(consts, 1)
            pool.memset(v0_ones[:, :, :, :], 1.0).then_inc(consts, 1)
            pool.memset(v1_ones[:, :, :, :, :], 1.0).then_inc(consts, 1)

            def split(j):
                staged_b, rest_b, part = job_views(j)
                pool.wait_ge(job_staged, j + 1)
                pool.wait_ge(job_split, j)
                pool.tensor_tensor(rest_b, staged_b, part[0], ALU.subtract).then_inc(job_rest, 1)
                pool.wait_ge(job_rest, j + 1)
                pool.tensor_copy(part[1], rest_b).then_inc(job_mid, 1)
                pool.wait_ge(job_mid, j + 1)
                pool.tensor_tensor(part[2], rest_b, part[1], ALU.subtract).then_inc(job_split, 1)

            pool.wait_ge(ld_mask, 16)
            pool.tensor_copy(mask_rows[:, 0, :], mask_all[:, 0, :]).then_inc(mask_rows_ready, 1)
            pool.wait_ge(consts, 5)

            def step(i, par, lay):
                l1, l2, lpv, lpr, lld = lay
                if lld == 0:
                    need(pool, max_ready, (i + 1) * BANKS)
                    alone(pool)
                    pool.tensor_copy(mask_rows[:, par, :], mask_all[:, at(i + 2), :].rearrange("q o s -> q (o s)")).then_inc(mask_rows_ready, 1)
                if l1 == 0:
                    need(pool, s2_ready, i * BANKS)
                    alone(pool)
                    pool.wait_ge(ld_mask, 16)
                    pool.tensor_copy(mask_sb[:, 1 - par, :], mask_all[:, at(i + 1), :].rearrange("q o s -> q (o s)")).then_inc(mask_ready, 1)
                if i_is(i, -1):
                    for j in range(JOBS_L0, JOBS_L0 + 2):
                        split(j)
                if l2 is not None:
                    need(pool, pv_ready, (i - 1) * 2)
                    alone(pool)
                    if l2 == 0:
                        pool.wait_ge(vctx_sb, NB)
                        pool.tensor_copy(v0_ones[:, par, :, 0:D0],
                                         v_ctx[:, at(i), 0:KV0 * D0].rearrange("p o (k d) -> p (o k) d", d=D0)).then_inc(v_ready, 1)
                    else:
                        pool.tensor_copy(v1_ones[:, par, 0, :, 0:D1],
                                         v_ctx[:, at(i - NB), KV0 * D0:].rearrange("p o (k d) -> p (o k) d", d=D1))
                        pool.wait_ge(vlat_sb, i - NB + 1)
                        alone(pool)
                        pool.tensor_copy(v1_ones[:, par, 1, :, 0:D1],
                                         v_lat[:, at(i - NB), :].rearrange("p o (k d) -> p (o k) d", d=D1)).then_inc(v_ready, 1)
                if i_is(i, 0):
                    pool.wait_ge(ld_resid, 16)
                    pool.wait_ge(ld_rows, 16)
                    for b in range(NB):
                        pool.tensor_tensor(resid0[:, b, :], resid0[:, b, :], bo0_row, ALU.add).then_inc(resid0_ready, 1)
                if i_is(i, 0) or i_is(i, 1):
                    split(JOBS0 - 2 + i)
                if lpr == 0:
                    pool.wait_ge(normed_ready, i - 1)
                    for resid, row in ((resid1, bo1_row), (resid2, b2_row)):
                        pool.tensor_tensor(resid[:, at(i - 2), :].rearrange("p o c -> p (o c)"), normed[:, par, :],
                                           row, ALU.add).then_inc(resid12_ready, 1)
                    for n in range(2):
                        j = (i - 2) * 2 + JOBS0 + n
                        pool.wait_ge(job_rest, j + 1)
                        alone(pool)
                        pool.tensor_copy(lat_part[n][1], rest_lat[:, n, :]).then_inc(job_mid, 1)
                        pool.wait_ge(job_mid, j + 1)
                        pool.tensor_tensor(lat_part[n][2], rest_lat[:, n, :], lat_part[n][1], ALU.subtract).then_inc(job_split, 1)
                if lpv is not None:
                    pool.wait_ge(moments, i)
                    alone(pool)
                    if lpv == 0:
                        pool.tensor_scalar(spread[:, :], mean_var[:, 1:2], EPS, None, ALU.add).then_inc(spread_ready, 1)
                    else:
                        pool.tensor_scalar(spread[:, :], mean_sq[:, :], 1.0 / H, EPS, ALU.mult, ALU.add).then_inc(spread_ready, 1)
                    pool.wait_ge(spread_ready, i)
                    pool.tensor_tensor(inv_std[:, :], spread[:, :], minus_half[:, :], ALU.pow).then_inc(std_ready, 1)

            iterate(pool, step)

        @block.tensor
        def _(pe):
            def project(out_ap, w, cols, m, n):
                for c in range(HC):
                    mm = pe.matmul(out_ap, w[:, c, m * 128:m * 128 + n], cols(c), start=(c == 0), stop=(c == HC - 1))
                return mm

            def job(j):
                kind, m, b, n = JOB[j]
                pe.wait_ge({"q0": ld_wq0, "k0": ld_wk0, "k1": ld_wk1}[kind], 16)
                pe.wait_ge((ld_x if kind == "q0" else ld_c)[b], 16)
                need(pe, job_staged, j - 3)
                w = {"q0": wq0_sb, "k0": wk0_sb, "k1": wk1_sb}[kind]
                src = x_cols if kind == "q0" else c_cols
                rows = KV0 * D0 if kind == "k0" else 128
                project(job_bank[j % 4][0:rows, 0:n * S], w, lambda c: src[:, c, b * S:(b + n) * S], m, rows).then_inc(job_mm, 1)

            def ctx_values(b):
                if b == 0:
                    pe.wait_ge(ld_wv, 16)
                need(pe, vctx_sb, b - 1)
                for c in range(HC):
                    mm = pe.matmul((m0_bank, m1_bank)[b % 2][:, 0:KV0 * D0 + H], c_cols[:, c, b * S:(b + 1) * S], wv_sb[:, c, :],
                                   start=(c == 0), stop=(c == HC - 1))
                mm.then_inc(vctx_mm, 1)

            def pass1(u, par, layer, k):
                if k % 4 == 0:
                    stack_need(pe, u, par, layer, k // 4)
                need(pe, max_ready, u * BANKS + (k - 1))
                dst = s1_bank[k % 2]
                if layer == 0:
                    for g in range(G0):
                        h = k * G0 + g
                        mm = pe.matmul(dst[:, g * S:(g + 1) * S], q_stack[0:MASK_ROW, par, h * S:(h + 1) * S],
                                       k_stack[0:MASK_ROW, par, k * S:(k + 1) * S], start=True, stop=True)
                else:
                    keys = k_stack[0:MAX_ROW, par, :].rearrange("r (c x) -> r c x", c=2)
                    for g in range(2):
                        col = col1(2 * k + g)
                        mm = pe.matmul(dst[:, g * 2 * S:(g + 1) * 2 * S].rearrange("p (c s) -> p c s", c=2),
                                       q_stack[0:MAX_ROW, par, col:col + S], keys[:, :, col:col + S], start=True, stop=True)
                mm.then_inc(s1_ready, 1)

            def maxima_turned(u, layer, lpr):
                heads = NH1 if layer else NH0
                pe.wait_ge(max_split, u + 1)
                if isinstance(u, int) and u == 0:
                    pe.wait_ge(consts, 2)
                    pe.wait_ge(vctx_sb, NB - 1)
                if lpr == 0:
                    pe.wait_ge(job_staged, (u - 3) * 2 + JOBS0 + 2)
                elif lpr == 1:
                    pe.wait_ge(xT_sb, u - 2)
                else:
                    need(pe, attnT_sb, u - 2)
                pe.matmul(m0_bank[0:3 * heads, 0:S], neg_parts[:, 0:3 * heads], ident_bf[:, :], start=True, stop=True).then_inc(maxT_ready, 1)

            def pass2(u, par, layer, k):
                if k == 0:
                    pe.wait_ge(max_rows, u * 16 + 16)
                    if isinstance(u, int) and u == 0:
                        pe.wait_ge(job_staged, JOBS0 - 2)
                need(pe, p_ready, u * BANKS + (k - 1))
                dst = s2_bank[k % 2]
                if layer == 0:
                    if k == 0:
                        pe.wait_ge(mask_ready, u + 1)
                    for g in range(G0):
                        pe.matmul(dst[:, g * S:(g + 1) * S], mask_sb[:, par, :], ident[:, :], is_transpose=True,
                                  start=(g == 0), stop=False)
                    mm = pe.matmul(dst[:, :], k_stack[0:ROWS, par, k * S:(k + 1) * S],
                                   q_stack[0:ROWS, par, k * 512:(k + 1) * 512], start=False, stop=True)
                else:
                    hg, c = k // 2, k % 2
                    for g in range(4):
                        col = col1(4 * hg + g)
                        mm = pe.matmul(dst[:, g * S:(g + 1) * S], k_stack[0:ROWS, par, c * NH1 * S + col:c * NH1 * S + col + S],
                                       q_stack[0:ROWS, par, col:col + S], start=True, stop=True)
                mm.then_inc(s2_ready, 1)

            def values(u, par, layer, half):
                pe.wait_ge(p_ready, u * BANKS + 4 * (half + 1))
                if half == 0:
                    pe.wait_ge(v_ready, u + 1)
                    if isinstance(u, int) and u == 0:
                        pe.wait_ge(job_staged, JOBS0)
                need(pe, o_sb, u * 2 + half)
                if layer == 0:
                    for j in range(4):
                        kv = 4 * half + j
                        mm = pe.matmul(pv_bank[32 * j:32 * j + 32, :], v0_ones[:, par, kv, :], probs[:, par, kv * 512:(kv + 1) * 512],
                                       start=True, stop=True)
                else:
                    for e in range(2):
                        hg = 2 * half + e
                        for c in range(2):
                            for j in range(4):
                                mm = pe.matmul(pv_bank[32 * j:32 * j + 32, e * S:(e + 1) * S], v1_ones[:, par, c, 4 * hg + j, :],
                                               probs[:, par, (2 * hg + c) * 512 + j * S:(2 * hg + c) * 512 + (j + 1) * S],
                                               start=(c == 0), stop=(c == 1))
                mm.then_inc(pv_ready, 1)

            def values_turned(u, layer, half):
                pe.wait_ge(o_sb, u * 2 + half + 1)
                need(pe, attn_ready, u * 2 + half)
                for g in range(2 if layer else 4):
                    mm = pe.transpose(ot_bank[:, g * S:(g + 1) * S], o_cols[:, half, g * S:(g + 1) * S], ident[:, :])
                mm.then_inc(oT_ready, 1)

            def attention_turned(u, more_max):
                pe.wait_ge(attn_ready, u * 2 + 2)
                if more_max:
                    pe.wait_ge(max_cols_sb, u + 3)
                else:
                    need(pe, xT_sb, u)
                for m in range(HC):
                    mm = pe.transpose(m0_bank[:, m * S:(m + 1) * S], attn[:, m * 128:(m + 1) * 128], ident[:, :])
                mm.then_inc(attnT_ready, 1)

            def out_projection(u, layer, lpr):
                pe.wait_ge(attnT_sb, u + 1)
                pe.wait_ge(ld_w1l if layer else ld_wo0, 32 if layer else 16)
                if lpr == 0:
                    pe.wait_ge(vlat_sb, u)
                elif lpr == 1:
                    pe.wait_ge(y_ready, u)
                w = wo1_sb if layer else wo0_sb
                for c in range(HC):
                    mm = pe.matmul(m1_bank[:, 0:H], attn_cols[:, c, :], w[:, c, :], start=(c == 0), stop=(c == HC - 1))
                mm.then_inc(wo_ready, 1)

            def result_turned(u, par):
                pe.wait_ge(normed_ready, u + 1)
                pe.wait_ge(attnT_sb, u + 1)
                for m in range(HC):
                    mm = pe.transpose(m0_bank[:, m * S:(m + 1) * S], normed[:, par, m * 128:(m + 1) * 128], ident[:, :])
                mm.then_inc(xT_ready, 1)

            def latent_queries(b):
                pe.wait_ge(xT_sb, b + 1)
                pe.wait_ge(ld_w1l, 32)
                need(pe, y_ready, b + 1)
                for m in range(HC):
                    mm = project(m1_bank[:, m * S:(m + 1) * S], wq1_sb, lambda c: latent_cols[:, c, :], m, 128)
                mm.then_inc(job_mm, 1)

            def latent_keys(b):
                for m in range(HC):
                    mm = project(m0_bank[:, m * S:(m + 1) * S], wk1_sb, lambda c: latent_cols[:, c, :], m, 128)
                mm.then_inc(job_mm, 1)

            def latent_values(b):
                pe.wait_ge(job_staged, b * 2 + JOBS0 + 1)
                for c in range(HC):
                    mm = pe.matmul(m1_bank[:, 0:H], latent_cols[:, c, :], wv_sb[:, c, KV0 * D0:], start=(c == 0), stop=(c == HC - 1))
                mm.then_inc(vlat_mm, 1)

            def hidden(n):
                half, m = n // FC, n % FC
                if n == 0:
                    pe.wait_ge(ld_mlp, 32)
                    pe.wait_ge(max_ready, UNITS * BANKS)
                    pe.wait_ge(p_ready, UNITS * BANKS)
                if m == 0:
                    pe.wait_ge(xT_sb, NB + (half + 1) * NB // 2)
                need(pe, h_ready, n - 3)
                project(h_bank[n % 4][:, :], w1_sb, lambda c: normed_cols[:, c, half * 512:(half + 1) * 512], m, 128).then_inc(h_mm, 1)

            def mlp_out(b):
                if b == 0:
                    pe.wait_ge(h_ready, FC)
                    pe.wait_ge(y_ready, UNITS)
                    pe.wait_ge(xT_sb, UNITS)
                    pe.wait_ge(o_sb, 2 * UNITS)
                    pe.wait_ge(attn_ready, 2 * UNITS)
                if b == NB // 2:
                    pe.wait_ge(h_ready, 2 * FC)
                need(pe, result_ready, b - 3)
                values = probs[:, b // 4, :].rearrange("p (m t) -> p m t", m=FC)
                for m in range(FC):
                    mm = pe.matmul(o_bank[b % 4][:, 0:H], values[:, m, (b % 4) * S:(b % 4 + 1) * S], w2_sb[:, m, :],
                                   start=(m == 0), stop=(m == FC - 1))
                mm.then_inc(mlp_mm, 1)

            pe.sem_inc(xT_ready, 2)
            pe.sem_inc(vlat_mm, 1)
            for j in range(JOBS_L0):
                job(j)

            def step(i, par, lay):
                l1, l2, lpv, lpr, lld = lay
                first = LEAD if l1 == 1 else 0
                banks = [range(BANKS)[first + 2 * k:first + 2 * k + 2] for k in range(BANKS)]
                for k in range(BANKS):
                    if l1 == 1 and k == 0:
                        for n in range(LEAD):
                            pass1(i + 1, 1 - par, l1, n)
                    if l2 is not None:
                        pass2(i, par, l2, k)
                    if k == 2 and lpr is not None:
                        result_turned(i - 2, par)
                    if k == 3 and lpr == 0:
                        latent_queries(i - 2)
                    if i_is(i, -1):
                        pass1(0, 0, 0, k)
                        if k == 7:
                            maxima_turned(0, 0, None)
                        ctx_values(k)
                        if k % 2:
                            job(JOBS_L0 + k // 2)
                    elif l1 is not None and banks[k]:
                        pass1(i + 1, 1 - par, l1, banks[k][0])
                    if lpv is not None:
                        if k in PV_SLOTS[lpv]:
                            values(i - 1, 1 - par, lpv, PV_SLOTS[lpv].index(k))
                        if k in TURN_SLOTS[lpv]:
                            values_turned(i - 1, lpv, TURN_SLOTS[lpv].index(k))
                    if not i_is(i, -1) and l1 is not None:
                        for n in banks[k][1:]:
                            pass1(i + 1, 1 - par, l1, n)
                    if k == 3 and lpr == 0:
                        latent_keys(i - 2)
                    if k == 4 and lpr == 0:
                        latent_values(i - 2)
                    if k == 5 and not i_is(i, -1) and l1 is not None:
                        maxima_turned(i + 1, l1, lpr)
                    if k == 6 and lpv is not None:
                        attention_turned(i - 1, l1 is not None)
                    if k == 7 and lpv is not None:
                        out_projection(i - 1, lpv, lpr)
                    for n in HIDDEN_AT.get((i, k), ()) if isinstance(i, int) else ():
                        hidden(n)

            iterate(pe, step)

            for n in range(FC, 2 * FC):
                hidden(n)
            for b in range(NB):
                mlp_out(b)

        @block.scalar
        def _(act):
            def stage(j):
                kind, m, b, n = JOB[j]
                rows = KV0 * D0 if kind == "k0" else 128
                if j == 0:
                    act.wait_ge(bias_scaled, 1)
                    act.wait_ge(ld_bias, 16)
                act.wait_ge(job_mm, j + 1)
                need(act, job_split, j - 2)
                need(act, job_stored[j % JOB_BUFS], stored_before(j))
                bias = {"q0": bq0_sb[:, m:m + 1], "k0": bk0_sb[0:rows], "k1": bk1_sb[:, m:m + 1]}[kind]
                scale = SCALE0 if kind == "q0" else 1.0
                src = job_bank[j % 4][0:rows, 0:n * S].rearrange("c (b t) -> c b t", b=n)
                staged_b, _, part = job_views(j)
                act.activation(staged_b, src, ACT.Identity, bias=bias, scale=scale)
                act.activation(part[0], src, ACT.Identity, bias=bias, scale=scale).then_inc(job_staged, 1)

            def stage_latents(b, n):
                j = b * 2 + (JOBS0 + n)
                act.wait_ge(job_mm, j + 1)
                act.wait_ge(job_split, j - 1)
                act.wait_ge(job_stored[n + 1], b * 48 + stored_jobs[n + 1])
                bias, scale = (bq1_sb, SCALE1) if n == 0 else (bk1_sb, 1.0)
                src = (m1_bank, m0_bank)[n]
                for m in range(HC):
                    act.activation(staged_lat[:, n, m * S:(m + 1) * S], src[:, m * S:(m + 1) * S], ACT.Identity,
                                   bias=bias[:, m:m + 1], scale=scale)
                    last = act.activation(lat_part[n][0][:, m * S:(m + 1) * S], src[:, m * S:(m + 1) * S], ACT.Identity,
                                          bias=bias[:, m:m + 1], scale=scale)
                last.then_inc(job_staged, 1)

            def maxima_out(u, layer):
                n = 3 * (NH1 if layer else NH0)
                act.wait_ge(maxT_ready, u + 1)
                need(act, max_rows, u * 16)
                act.copy(max_cols[0:n, :], m0_bank[0:n, 0:S]).then_inc(max_cols_sb, 1)

            def exponentials(u, par, k):
                act.wait_ge(s2_ready, u * BANKS + (k + 1))
                if k % 4 == 0:
                    need(act, pv_ready, (u - 2) * 2 + k // 4 + 1)
                act.activation(probs[:, par, k * 512:(k + 1) * 512], s2_bank[k % 2][:, :], ACT.Exp).then_inc(p_ready, 1)

            def values_out(u, layer, half):
                n = 256 if layer else 512
                act.wait_ge(pv_ready, u * 2 + half + 1)
                need(act, oT_ready, u * 2 + (half - 1))
                act.copy(o_cols[:, half, 0:n], pv_bank[:, 0:n]).then_inc(o_sb, 1)

            def attention_out(u):
                act.wait_ge(attnT_ready, u + 1)
                need(act, wo_ready, u)
                act.copy(attn_cols[:, :, :], m0_bank[:, 0:H].rearrange("p (m t) -> p m t", m=HC)).then_inc(attnT_sb, 1)

            def result_out(u, layer):
                act.wait_ge(xT_ready, u + 3)
                src = m0_bank[:, 0:H].rearrange("p (m t) -> p m t", m=HC)
                if layer == 0:
                    need(act, vlat_mm, u + 1)
                    act.copy(latent_cols[:, :, :], src).then_inc(xT_sb, 1)
                else:
                    act.copy(normed_cols[:, :, bass.ds((u - NB) * S, S)], src).then_inc(xT_sb, 1)

            def query_rows(par):
                act.activation(q_stack[96:128, par, :], ident[96:128, 0:1].broadcast_to([32, NH0 * S]), ACT.Identity,
                               scale=0.0, bias=1.0).then_inc(query_row_set, 1)

            act.wait_ge(consts, 1)
            query_rows(0)
            for j in range(3):
                stage(j)
            query_rows(1)
            for j in range(3, 6):
                stage(j)

            def gelu(n):
                act.wait_ge(h_mm, n + 1)
                if n % FC == 0:
                    act.wait_ge(pv_ready, 2 * UNITS - (2 if n == 0 else 0))
                half, m = n // FC, n % FC
                act.activation(probs[:, half, m * 512:(m + 1) * 512], h_bank[n % 4][:, :], ACT.Gelu_apprx_tanh,
                               bias=b1_sb[:, m:m + 1]).then_inc(h_ready, 1)

            def constant_rows(par):
                n0, n1 = KV0 * S, 2 * NH1 * S
                some = ident[96:128, 0:1]
                act.activation(k_stack[96:128, par, n0:n1], some.broadcast_to([32, n1 - n0]), ACT.Identity,
                               scale=0.0, bias=1.0).then_inc(rows_one, 1)
                act.wait_ge(rows_one, par + 1)
                act.activation(k_stack[MASK_ROW:MASK_ROW + 1, par, n0:n1], some[0:1].broadcast_to([1, n1 - n0]), ACT.Identity,
                               scale=0.0, bias=0.0).then_inc(rows_set, 1)

            def step(i, par, lay):
                l1, l2, lpv, lpr, lld = lay
                for k in range(BANKS):
                    if l2 is not None:
                        exponentials(i, par, k)
                    if i_is(i, -1) and k in (0, 4):
                        constant_rows(k // 4)
                    elif i_is(i, -1) and k < 7:
                        stage(5 + k - k // 4)
                    if i_is(i, 0) and k in (2, 7):
                        stage(JOBS0 - (2 if k == 2 else 1))
                    if k == 2 and lpr is not None:
                        result_out(i - 2, lpr)
                    if lpv is not None and k in PV_SLOTS[lpv]:
                        values_out(i - 1, lpv, PV_SLOTS[lpv].index(k))
                    if k == 3 and lpr == 0:
                        stage_latents(i - 2, 0)
                    if k == 4 and lpr == 0:
                        stage_latents(i - 2, 1)
                    if k == (7 if i_is(i, -1) else 5) and l1 is not None:
                        maxima_out(i + 1, l1)
                    if k == 6 and lpv is not None:
                        attention_out(i - 1)
                    for n in HIDDEN_AT.get((i, k), ()) if isinstance(i, int) else ():
                        gelu(n)

            iterate(act, step)
            for n in range(FC, 2 * FC):
                gelu(n)

        @block.vector
        def _(dve):
            def init_stacks(par):
                n = KV0 * S
                dve.memset(k_stack[0:96, par, 0:n].bitcast(F32), 0.0)
                dve.memset(k_stack[96:128, par, 0:n], 1.0).then_inc(stacks_ones, 1)
                dve.memset(q_stack[0:96, par, :].bitcast(F32), 0.0)
                dve.wait_ge(stacks_ones, par + 1)
                dve.memset(k_stack[MASK_ROW:MASK_ROW + 1, par, 0:n].bitcast(F32), 0.0).then_inc(stacks_init, 1)

            def split(j):
                staged_b, rest_b, part = job_views(j)
                dve.wait_ge(job_staged, j + 1)
                dve.tensor_tensor(rest_b, staged_b, part[0], ALU.subtract).then_inc(job_rest, 1)
                dve.wait_ge(job_rest, j + 1)
                dve.tensor_copy(part[1], rest_b).then_inc(job_mid, 1)
                dve.wait_ge(job_mid, j + 1)
                dve.tensor_tensor(part[2], rest_b, part[1], ALU.subtract).then_inc(job_split, 1)

            def latent_rest(b, n):
                j = b * 2 + (JOBS0 + n)
                dve.wait_ge(job_staged, j + 1)
                dve.wait_ge(job_split, j - 1)
                dve.tensor_tensor(rest_lat[:, n, :], staged_lat[:, n, :], lat_part[n][0], ALU.subtract).then_inc(job_rest, 1)

            def context_values(b):
                dve.wait_ge(vctx_mm, b + 1)
                if b == 0:
                    dve.wait_ge(ld_bv, 16)
                n = KV0 * D0 + H
                dve.tensor_tensor(v_ctx[:, b, :], (m0_bank, m1_bank)[b % 2][:, 0:n], bv_row, ALU.add).then_inc(vctx_sb, 1)

            def maxima(u, par, layer, k):
                dve.wait_ge(s1_ready, u * BANKS + (k + 1))
                if k == 0:
                    need(dve, max_split, u)
                    if layer == 0:
                        dve.wait_ge(mask_rows_ready, u + 1)
                if layer == 0:
                    alone(dve)
                    for g in range(G0):
                        h = k * G0 + g
                        last = dve.tensor_tensor_reduce(s1_bank[k % 2][:, g * S:(g + 1) * S], s1_bank[k % 2][:, g * S:(g + 1) * S], mask_rows[:, par, :],
                                                        1.0, LOWEST, ALU.add, ALU.max, row_max[:, h:h + 1])
                    last.then_inc(max_ready, 1)
                else:
                    first = col1(2 * k) // S
                    dve.tensor_reduce(row_max[:, first:first + 2], s1_bank[k % 2][:, :].rearrange("p (h s) -> p h s", h=2),
                                      AX.X, ALU.max).then_inc(max_ready, 1)

            def normalise(u, layer, half):
                dve.wait_ge(oT_ready, u * 2 + half + 1)
                if half == 0:
                    need(dve, attnT_ready, u)
                if layer == 0:
                    turned = ot_bank[:, :].rearrange("q (g j e) -> q j g e", g=G0, j=4)
                    dst = attn[:, half * 128:(half + 1) * 128].rearrange("q (j g d) -> q j g d", j=4, g=G0)
                    d, n = D0, 16
                    inv = inv_sum[:, half, 0:16].rearrange("q (j g a) -> q j g a", j=4, g=G0)
                    shape = [128, 4, G0, D0]
                else:
                    turned = ot_bank[:, 0:2 * S].rearrange("q (e j c) -> q e j c", e=2, j=4)
                    dst = attn[:, half * 128:(half + 1) * 128].rearrange("q (e j d) -> q e j d", e=2, j=4)
                    d, n = D1, 8
                    inv = inv_sum[:, half, 0:8].rearrange("q (e j a) -> q e j a", e=2, j=4)
                    shape = [128, 2, 4, D1]
                dve.reciprocal(inv, turned[:, :, :, d:d + 1]).then_inc(inv_ready, 1)
                dve.wait_ge(inv_ready, u * 2 + half + 1)
                dve.tensor_tensor(dst, turned[:, :, :, 0:d], inv.broadcast_to(shape), ALU.mult).then_inc(attn_ready, 1)

            def residual_sum(u, par, layer):
                dve.wait_ge(wo_ready, u + 1)
                need(dve, normed_ready, u)
                if layer == 0:
                    dve.wait_ge(resid0_ready, NB)
                    dve.tensor_tensor(y[:, :], m1_bank[:, 0:H], resid0[:, at(u), :].rearrange("q o c -> q (o c)"), ALU.add).then_inc(y_ready, 1)
                    dve.wait_ge(y_ready, u + 1)
                    dve.bn_stats(stats[:, :], y[:, :]).then_inc(bn_done, 1)
                    dve.wait_ge(bn_done, u + 1)
                    alone(dve)
                    dve.bn_aggr(mean_var[:, :], stats[:, :]).then_inc(moments, 1)
                else:
                    dve.wait_ge(resid12_ready, 2 * NB + 3)
                    dve.tensor_tensor(y[:, :], m1_bank[:, 0:H], resid1[:, at(u - NB), :].rearrange("p o c -> p (o c)"), ALU.add).then_inc(y_ready, 1)
                    dve.wait_ge(y_ready, u + 1)
                    dve.tensor_tensor_reduce(y_scaled[:, :], y[:, :], y[:, :], 1.0, 0.0, ALU.mult, ALU.add, mean_sq[:, :]).then_inc(moments, 1)

            def split_maxima(u, layer):
                heads = NH1 if layer else NH0
                maxima_of_unit, rest_of_max = row_max[:, 0:heads], neg_rest[:, 0:heads]
                part = [neg_parts[:, p * heads:(p + 1) * heads] for p in range(3)]
                dve.wait_ge(max_ready, u * BANKS + BANKS)
                need(dve, maxT_ready, u)
                dve.tensor_scalar(part[0], maxima_of_unit, -1.0, None, ALU.mult).then_inc(neg_ready, 1)
                dve.wait_ge(neg_ready, u + 1)
                dve.scalar_tensor_tensor(rest_of_max, maxima_of_unit, -1.0, part[0], ALU.mult, ALU.subtract).then_inc(neg_rest_ready, 1)
                dve.wait_ge(neg_rest_ready, u + 1)
                dve.tensor_copy(part[1], rest_of_max).then_inc(neg_mid_ready, 1)
                dve.wait_ge(neg_mid_ready, u + 1)
                dve.tensor_tensor(part[2], rest_of_max, part[1], ALU.subtract).then_inc(max_split, 1)

            def norm(u, par, layer):
                dve.wait_ge(std_ready, u + 1)
                dve.wait_ge(xT_ready, u + 1)
                if layer == 0:
                    dve.wait_ge(resid12_ready, u * 2 + 1)
                    dve.scalar_tensor_tensor(y_scaled[:, :], y[:, :], mean_var[:, 0:1], gamma_row, ALU.subtract, ALU.mult).then_inc(scaled_ready, 1)
                    dve.wait_ge(scaled_ready, u + 1)
                    dve.scalar_tensor_tensor(normed[:, par, :], y_scaled[:, :], inv_std[:, 0:1], beta_row, ALU.mult, ALU.add).then_inc(normed_ready, 1)
                else:
                    dve.scalar_tensor_tensor(normed[:, par, :], y[:, :], inv_std[:, 0:1], post_row, ALU.mult, ALU.mult).then_inc(normed_ready, 1)

            init_stacks(0)
            for j in range(3):
                split(j)
            init_stacks(1)
            for j in range(3, 6):
                split(j)

            def step(i, par, lay):
                l1, l2, lpv, lpr, lld = lay
                for k in range(BANKS):
                    if i_is(i, -1):
                        maxima(0, 0, 0, k)
                        if k == 7:
                            split_maxima(0, 0)
                        context_values(k)
                        if 3 <= k < 6:
                            split(3 + k)
                    elif l1 is not None and k < 4:
                        maxima(i + 1, 1 - par, l1, 2 * k)
                        maxima(i + 1, 1 - par, l1, 2 * k + 1)
                    if k == 0 and lpr is not None:
                        norm(i - 2, par, lpr)
                    if k == 3 and not i_is(i, -1) and l1 is not None:
                        split_maxima(i + 1, l1)
                    if lpv is not None and k in TURN_SLOTS[lpv]:
                        normalise(i - 1, lpv, TURN_SLOTS[lpv].index(k))
                    if k == 4 and lpr == 0:
                        latent_rest(i - 2, 0)
                        latent_rest(i - 2, 1)
                    if k == 5 and lpr == 0:
                        dve.wait_ge(vlat_mm, i)
                        dve.tensor_tensor(v_lat[:, at(i - 2), :].rearrange("p o c -> p (o c)"), m1_bank[:, 0:H],
                                          bv_row[:, KV0 * D0:], ALU.add).then_inc(vlat_sb, 1)
                    if k == 7 and lpv is not None:
                        residual_sum(i - 1, 1 - par, lpv)
                if i_is(i, -1):
                    dve.wait_ge(ld_keym, 16)
                    dve.tensor_scalar(key_bias[:, :], key_mask_sb[:, :], 0.0, MASKED, ALU.is_equal, ALU.mult).then_inc(key_bias_ready, 1)

            iterate(dve, step)
            for b in range(NB):
                dve.wait_ge(mlp_mm, b + 1)
                need(dve, stored[b % 2], 16 * (b // 2))
                dve.tensor_tensor(result[:, b % 2, :], [m0_bank, m1_bank, pv_bank, ot_bank][b % 4][:, 0:H], resid2[:, b, :], ALU.add).then_inc(result_ready, 1)


def stored_before(j):
    return sum(16 * (BLOCKS if JOB[e][0] == "k1" else 1) for e in range(j % JOB_BUFS, j, JOB_BUFS))


def pieces(tile, widths):
    starts = [sum(widths[:n]) for n in range(len(widths))]
    return [tile[:, a:a + w] for a, w in zip(starts, widths)]


def col1(h):
    return HALF_COL1[h // 8] + (h % 8) * S


def i_is(i, n):
    return isinstance(i, int) and i == n


def kernel(**inputs):
    import numpy as np
    import concourse.bacc as bacc
    from concourse.bass_utils import run_bass_kernel_spmd

    a = {k: np.asarray(v) for k, v in inputs.items()}

    def cols(w):
        return np.ascontiguousarray(w.reshape(-1, 128, w.shape[1]).transpose(1, 0, 2))

    def tokens(v):
        return cols(v.reshape(T, H).T)

    def d_major(w, heads, d):
        return w.reshape(-1, heads, d).transpose(0, 2, 1).reshape(-1, heads * d)

    kv_w = a["L1_xattn_kv_w"].reshape(H, NH1, D1, 2)
    kv_b = a["L1_xattn_kv_b"].reshape(1, NH1, D1, 2)

    def column(v):
        return cols(v.reshape(-1, 1))[:, :, 0]

    key_bias0 = np.zeros((128, 1), np.float32)
    key_bias0[:KV0 * D0, 0] = d_major(a["L0_xattn_bk"], KV0, D0)[0]
    biases = [column(d_major(a["L0_xattn_bq"], NH0, D0)), key_bias0, column(d_major(a["L1_xattn_q_b"], NH1, D1)),
              column(d_major(kv_b[..., 0].reshape(1, H), NH1, D1)), column(a["L1_xattn_mlp_b1"])]
    rows = [a["L0_xattn_bv"], kv_b[..., 1], a["L0_xattn_bo"], a["L0_xattn_gamma"], a["L0_xattn_beta"],
            a["L1_xattn_out_b"], a["L1_xattn_postnorm_w"], a["L1_xattn_mlp_b2"]]
    arrays = {
        "xT": tokens(a["x"]), "x": a["x"], "cT": tokens(a["ctx_2048"]),
        "mask": a["mask_Bx1xSxS2_ff0"].reshape(NB, S, S), "key_mask": a["mask_BxS2_ik0"],
        "biases": np.concatenate(biases, axis=1), "rows": np.concatenate([v.reshape(1, -1) for v in rows], axis=1),
        "wq0": cols(d_major(a["L0_xattn_Wq"], NH0, D0)), "wk0": cols(d_major(a["L0_xattn_Wk"], KV0, D0)),
        "wv": cols(np.concatenate([a["L0_xattn_Wv"], kv_w[..., 1].reshape(H, H)], axis=1)),
        "wo0": cols(a["L0_xattn_Wo"]), "wq1": cols(d_major(a["L1_xattn_q_w"], NH1, D1)),
        "wk1": cols(d_major(kv_w[..., 0].reshape(H, H), NH1, D1)), "wo1": cols(a["L1_xattn_out_w"]),
        "w1": cols(a["L1_xattn_mlp_w1"]), "w2": cols(a["L1_xattn_mlp_w2"]),
    }
    nc = bacc.Bacc("TRN2", target_bir_lowering=False, num_devices=1)
    args, feed = [], {}
    for name, v in arrays.items():
        v = np.ascontiguousarray(v)
        feed[f"in_{name}"] = v
        args.append(nc.dram_tensor(f"in_{name}", v.shape, mybir.dt.from_np(v.dtype), kind="ExternalInput").ap())
    out = nc.dram_tensor("out_0", (NB, S, H), F32, kind="ExternalOutput").ap()
    cross_attention_layers(nc, *args, out)
    r = run_bass_kernel_spmd(nc, [feed], core_ids=[0])
    return r.results[0]["out_0"]
```
